# Optimizing a Trainium2 kernel written in Bass

```python
import numpy as np
import jax
import jax.numpy as jnp

def _softmax(x, axis=-1):
    return jax.nn.softmax(x, axis=axis)

def _gelu(x):
    return jax.nn.gelu(x, approximate=True)

def _silu(x):
    return jax.nn.silu(x)

def _sigmoid(x):
    return jax.nn.sigmoid(x)

def _layernorm(x, axis=-1, eps=1e-05):
    m = jnp.mean(x, axis=axis, keepdims=True)
    v = jnp.var(x, axis=axis, keepdims=True)
    return (x - m) / jnp.sqrt(v + eps)

def _scatter_add(tgt, idx, src, axis=0):
    return tgt.at[idx].add(src)

def _segment_sum(src, seg, n):
    return jax.ops.segment_sum(src, seg, n)
kernel_name = 'mk_vit_tower_d2_tok_img1024_r4_df1cd7'

def setup_inputs(seed: int=0):
    np.random.seed(seed)
    _w = jnp.asarray

    def _rec_inputs():
        import jax
        import jax.numpy as jnp
        _rk = jax.random.key(seed)
        x = -0.00150118 + 0.499729 * jax.random.normal(jax.random.fold_in(_rk, 1), (8, 256, 64, 2), jnp.float32)
        return x
    x = _rec_inputs()

    def _L0_tok_setup():
        import jax, jax.numpy as jnp
        import numpy as np
        import math
        H = 256
        N = 64
        CH = 1
        SEQ_L = 256
        key = jax.random.key(seed)
        k1, k2, k3, k4 = jax.random.split(key, 4)
        log_dt = jax.random.uniform(k1, (H,), dtype=jnp.float32, minval=math.log(0.001), maxval=math.log(0.1))
        inv_A_real = jnp.log(0.5 * jnp.ones((H, N), jnp.float32)) + 0.1 * jax.random.normal(k2, (H, N), dtype=jnp.float32)
        A_imag = jnp.broadcast_to(math.pi * jnp.arange(N, dtype=jnp.float32), (H, N)).copy()
        B_ri = jax.random.normal(k3, (H, N, 2), dtype=jnp.float32) * 0.5
        C_ri = jax.random.normal(k4, (CH, H, N, 2), dtype=jnp.float32) * 0.5
        return {'log_dt': log_dt, 'inv_A_real': inv_A_real, 'A_imag': A_imag, 'B_ri': B_ri, 'C_ri': C_ri, 'L': SEQ_L}
    _L0_tok_all = _L0_tok_setup()
    _L0_tok_in = {k: v for k, v in _L0_tok_all.items() if k in ('log_dt', 'inv_A_real', 'A_imag', 'B_ri')}
    del _L0_tok_all

    def _L0_attn_setup():
        import jax, jax.numpy as jnp
        import numpy as np
        B_, S_, H_, I_, N_, K_ = (2, 512, 256, 512, 16, 4)

        def _layernorm(x, g, b, eps=1e-05):
            mu = jnp.mean(x, axis=-1, keepdims=True)
            var = jnp.mean((x - mu) ** 2, axis=-1, keepdims=True)
            return (x - mu) * jax.lax.rsqrt(var + eps) * g + b
        key = jax.random.key(seed)
        ks = jax.random.split(key, 6)
        return {'x': jax.random.normal(ks[0], (B_, S_, H_), jnp.float32), 'W_in': jax.random.normal(ks[1], (H_, 2 * I_), jnp.float32) * H_ ** (-0.5), 'conv_w': jax.random.normal(ks[2], (I_, 1, K_), jnp.float32) * K_ ** (-0.5), 'ln_gamma': jnp.ones((I_,), jnp.float32), 'ln_beta': jnp.zeros((I_,), jnp.float32), 'W_xproj': jax.random.normal(ks[3], (I_, 2 * N_ + 1), jnp.float32) * I_ ** (-0.5), 'A_param': jax.random.normal(ks[4], (I_, N_), jnp.float32) * 0.1, 'D': jnp.ones((I_,), jnp.float32), 'W_out': jax.random.normal(ks[5], (I_, H_), jnp.float32) * I_ ** (-0.5)}
    _L0_attn_all = _L0_attn_setup()
    _L0_attn_in = {k: v for k, v in _L0_attn_all.items() if k in ('W_in', 'conv_w', 'ln_gamma', 'ln_beta', 'W_xproj', 'A_param', 'D', 'W_out')}
    del _L0_attn_all

    def _L0_ffn_setup():
        import jax, jax.numpy as jnp
        import numpy as np
        B, S, D = (4, 512, 256)
        E, F = (8, 1024)
        key = jax.random.key(seed)
        ks = jax.random.split(key, 5)
        x = jax.random.normal(ks[0], (B, S, D), dtype=jnp.float32)
        switch_w = jax.random.normal(ks[1], (D, E), dtype=jnp.float32) * D ** (-0.5)
        switch_b = jnp.zeros((E,), dtype=jnp.float32)
        w1 = jax.random.normal(ks[2], (E, D, F), dtype=jnp.float32) * D ** (-0.5)
        b1 = jnp.zeros((E, F), dtype=jnp.float32)
        w2 = jax.random.normal(ks[3], (E, F, D), dtype=jnp.float32) * F ** (-0.5)
        b2 = jnp.zeros((E, D), dtype=jnp.float32)
        return {'x': x, 'switch_w': switch_w, 'switch_b': switch_b, 'w1': w1, 'b1': b1, 'w2': w2, 'b2': b2}
    _L0_ffn_all = _L0_ffn_setup()
    _L0_ffn_in = {k: v for k, v in _L0_ffn_all.items() if k in ('switch_w', 'switch_b', 'w1', 'b1', 'w2', 'b2')}
    del _L0_ffn_all

    def _L1_attn_setup():
        import jax, jax.numpy as jnp
        import numpy as np
        D_MODEL = 256
        N_HEADS = 16
        D_K = D_MODEL // N_HEADS
        THETA = 10000.0
        BATCH = 1
        SEQ = 1024

        def _rope(x, pos, inv_freq):
            angles = pos[:, None].astype(jnp.float32) * inv_freq
            cos = jnp.repeat(jnp.cos(angles), 2, axis=-1)
            sin = jnp.repeat(jnp.sin(angles), 2, axis=-1)
            x_rot = jnp.stack([-x[..., 1::2], x[..., 0::2]], axis=-1).reshape(x.shape)
            return x * cos + x_rot * sin
        key = jax.random.key(seed)
        ks = jax.random.split(key, 5)
        std = (2.0 / (D_MODEL + D_MODEL)) ** 0.5
        mk = lambda k: jax.random.truncated_normal(k, -3.0, 3.0, (D_MODEL, D_MODEL), jnp.float32) * std
        return {'x': jax.random.normal(ks[0], (BATCH, SEQ, D_MODEL), jnp.float32), 'Wq': mk(ks[1]), 'Wk': mk(ks[2]), 'Wv': mk(ks[3]), 'Wo': mk(ks[4])}
    _L1_attn_all = _L1_attn_setup()
    _L1_attn_in = {k: v for k, v in _L1_attn_all.items() if k in ('Wq', 'Wk', 'Wv', 'Wo')}
    del _L1_attn_all

    def _L1_ffn_setup():
        import jax, jax.numpy as jnp
        import numpy as np
        B, T, H, F, E, TOPK = (4, 256, 256, 1024, 8, 2)

        def _moe_forward(x, rw, rb, w1, b1, w2, b2, sw1, sb1, sw2, sb2):
            Bb, Tt, Hh = x.shape
            N = Bb * Tt
            Ee = rw.shape[0]
            cap = max(1, int(N / Ee * 1.0))
            xf = x.reshape(N, Hh)
            logits = xf @ rw.T + rb
            g_soft = jax.nn.softmax(logits, axis=-1)
            _, idx = jax.lax.top_k(g_soft, TOPK)
            primary, second = (idx[:, 0], idx[:, 1])
            ohp = jax.nn.one_hot(primary, Ee, dtype=jnp.int32)
            posp = jnp.cumsum(ohp, axis=0) - ohp
            pos_tok = jnp.take_along_axis(posp, primary[:, None], 1)[:, 0]
            keep_primary = pos_tok < cap
            used = jnp.minimum(ohp.sum(axis=0), cap)
            overflow = ~keep_primary
            ohs = jax.nn.one_hot(second, Ee, dtype=jnp.int32) * overflow[:, None].astype(jnp.int32)
            poss = jnp.cumsum(ohs, axis=0) - ohs
            pos2 = jnp.take_along_axis(poss, second[:, None], 1)[:, 0]
            take2 = overflow & (used[second] + pos2 < cap)
            assign = jnp.where(keep_primary, primary, jnp.where(take2, second, -1))
            overflow = overflow & ~take2
            h = jax.nn.gelu(jnp.einsum('nh,ehf->enf', xf, w1) + b1[:, None, :], approximate=False)
            stack = jnp.einsum('enf,efh->enh', h, w2) + b2[:, None, :]
            one_hot_a = jax.nn.one_hot(assign, Ee, dtype=stack.dtype)
            y = jnp.einsum('enh,ne->nh', stack, one_hot_a)
            y_fb = jax.nn.gelu(xf @ sw1 + sb1, approximate=False) @ sw2 + sb2
            y = jnp.where(overflow[:, None], y_fb, y)
            return y.reshape(Bb, Tt, Hh)
        key = jax.random.key(seed)
        ks = jax.random.split(key, 12)
        s = 0.02
        return {'x': jax.random.normal(ks[0], (B, T, H), dtype=jnp.float32), 'rw': jax.random.normal(ks[1], (E, H), dtype=jnp.float32) * s, 'rb': jnp.zeros((E,), dtype=jnp.float32), 'w1': jax.random.normal(ks[2], (E, H, F), dtype=jnp.float32) * s, 'b1': jnp.zeros((E, F), dtype=jnp.float32), 'w2': jax.random.normal(ks[3], (E, F, H), dtype=jnp.float32) * s, 'b2': jnp.zeros((E, H), dtype=jnp.float32), 'sw1': jax.random.normal(ks[4], (H, F), dtype=jnp.float32) * s, 'sb1': jnp.zeros((F,), dtype=jnp.float32), 'sw2': jax.random.normal(ks[5], (F, H), dtype=jnp.float32) * s, 'sb2': jnp.zeros((H,), dtype=jnp.float32)}
    _L1_ffn_all = _L1_ffn_setup()
    _L1_ffn_in = {k: v for k, v in _L1_ffn_all.items() if k in ('rw', 'rb', 'w1', 'b1', 'w2', 'b2', 'sw1', 'sb1', 'sw2', 'sb2')}
    del _L1_ffn_all
    return {'x': x, 'L0_tok_log_dt': _L0_tok_in['log_dt'], 'L0_tok_inv_A_real': _L0_tok_in['inv_A_real'], 'L0_tok_A_imag': _L0_tok_in['A_imag'], 'L0_tok_B_ri': _L0_tok_in['B_ri'], 'L0_attn_W_in': _L0_attn_in['W_in'], 'L0_attn_conv_w': _L0_attn_in['conv_w'], 'L0_attn_ln_gamma': _L0_attn_in['ln_gamma'], 'L0_attn_ln_beta': _L0_attn_in['ln_beta'], 'L0_attn_W_xproj': _L0_attn_in['W_xproj'], 'L0_attn_A_param': _L0_attn_in['A_param'], 'L0_attn_D': _L0_attn_in['D'], 'L0_attn_W_out': _L0_attn_in['W_out'], 'L0_ffn_switch_w': _L0_ffn_in['switch_w'], 'L0_ffn_switch_b': _L0_ffn_in['switch_b'], 'L0_ffn_w1': _L0_ffn_in['w1'], 'L0_ffn_b1': _L0_ffn_in['b1'], 'L0_ffn_w2': _L0_ffn_in['w2'], 'L0_ffn_b2': _L0_ffn_in['b2'], 'L1_attn_Wq': _L1_attn_in['Wq'], 'L1_attn_Wk': _L1_attn_in['Wk'], 'L1_attn_Wv': _L1_attn_in['Wv'], 'L1_attn_Wo': _L1_attn_in['Wo'], 'L1_ffn_rw': _L1_ffn_in['rw'], 'L1_ffn_rb': _L1_ffn_in['rb'], 'L1_ffn_w1': _L1_ffn_in['w1'], 'L1_ffn_b1': _L1_ffn_in['b1'], 'L1_ffn_w2': _L1_ffn_in['w2'], 'L1_ffn_b2': _L1_ffn_in['b2'], 'L1_ffn_sw1': _L1_ffn_in['sw1'], 'L1_ffn_sb1': _L1_ffn_in['sb1'], 'L1_ffn_sw2': _L1_ffn_in['sw2'], 'L1_ffn_sb2': _L1_ffn_in['sb2']}

def reference(x, L0_tok_log_dt, L0_tok_inv_A_real, L0_tok_A_imag, L0_tok_B_ri, L0_attn_W_in, L0_attn_conv_w, L0_attn_ln_gamma, L0_attn_ln_beta, L0_attn_W_xproj, L0_attn_A_param, L0_attn_D, L0_attn_W_out, L0_ffn_switch_w, L0_ffn_switch_b, L0_ffn_w1, L0_ffn_b1, L0_ffn_w2, L0_ffn_b2, L1_attn_Wq, L1_attn_Wk, L1_attn_Wv, L1_attn_Wo, L1_ffn_rw, L1_ffn_rb, L1_ffn_w1, L1_ffn_b1, L1_ffn_w2, L1_ffn_b2, L1_ffn_sw1, L1_ffn_sb1, L1_ffn_sw2, L1_ffn_sb2):
    import jax
    import jax.numpy as jnp

    def _L0_tok_ref(log_dt, inv_A_real, A_imag, B_ri, C_ri, L):
        import jax, jax.numpy as jnp
        import numpy as np
        import math
        H = 256
        N = 64
        CH = 1
        SEQ_L = 256
        dt = jnp.exp(log_dt)
        A = -jnp.exp(inv_A_real) + 1j * A_imag
        B = B_ri[..., 0] + 1j * B_ri[..., 1]
        C = C_ri[..., 0] + 1j * C_ri[..., 1]
        dtA = A * dt[:, None]
        dA = (1.0 + dtA / 2) / (1.0 - dtA / 2)
        C_term = C * B[None]
        log_dA = jnp.log(dA)
        V = jnp.exp(log_dA[:, :, None] * jnp.arange(L))
        K = 2.0 * jnp.einsum('chn,hnl->chl', C_term, V).real
        return K.astype(jnp.float32)

    def _L0_attn_ref(x, W_in, conv_w, ln_gamma, ln_beta, W_xproj, A_param, D, W_out):
        import jax, jax.numpy as jnp
        import numpy as np
        B_, S_, H_, I_, N_, K_ = (2, 512, 256, 512, 16, 4)

        def _layernorm(x, g, b, eps=1e-05):
            mu = jnp.mean(x, axis=-1, keepdims=True)
            var = jnp.mean((x - mu) ** 2, axis=-1, keepdims=True)
            return (x - mu) * jax.lax.rsqrt(var + eps) * g + b
        b, s, _ = x.shape
        n = A_param.shape[1]
        xz = x @ W_in
        xc, z = jnp.split(xz, 2, axis=-1)
        xc = jax.lax.conv_general_dilated(xc.transpose(0, 2, 1), conv_w, window_strides=(1,), padding=[(conv_w.shape[-1] - 1, 0)], feature_group_count=conv_w.shape[0], dimension_numbers=('NCH', 'OIH', 'NCH')).transpose(0, 2, 1)
        xc = jax.nn.silu(xc)
        xc = _layernorm(xc, ln_gamma, ln_beta)
        xp = xc @ W_xproj
        delta = jnp.clip(jax.nn.softplus(xp[..., :1]), 1e-06, 10.0)
        Bm = xp[..., 1:1 + n]
        Cm = xp[..., 1 + n:]
        A = -jnp.clip(jax.nn.softplus(A_param), 0.1, 10.0)
        decay = jnp.clip(jnp.exp(delta[..., None] * A[None, None]), 1e-06, 1.0)
        y = xc * jnp.einsum('bsn,bsin->bsi', Bm * Cm, decay)
        y = y + xc * D
        return y * jax.nn.silu(z) @ W_out

    def _L0_ffn_ref(x, switch_w, switch_b, w1, b1, w2, b2):
        import jax, jax.numpy as jnp
        import numpy as np
        B, S, D = (4, 512, 256)
        E, F = (8, 1024)
        b, s, d = x.shape
        t = x.reshape(-1, d)
        logits = t @ switch_w + switch_b
        route_prob = jax.nn.softmax(logits, axis=-1)
        route_prob_max = jnp.max(route_prob, axis=-1)
        routes = jnp.argmax(route_prob, axis=-1)
        out = jnp.zeros_like(t)
        n_experts = w1.shape[0]
        for e in range(n_experts):
            h = jax.nn.gelu(t @ w1[e] + b1[e])
            y = h @ w2[e] + b2[e]
            mask = (routes == e)[:, None]
            out = jnp.where(mask, y, out)
        out = out * route_prob_max[:, None]
        return out.reshape(b, s, d)

    def _L1_attn_ref(x, Wq, Wk, Wv, Wo):
        import jax, jax.numpy as jnp
        import numpy as np
        D_MODEL = 256
        N_HEADS = 16
        D_K = D_MODEL // N_HEADS
        THETA = 10000.0
        BATCH = 1
        SEQ = 1024

        def _rope(x, pos, inv_freq):
            angles = pos[:, None].astype(jnp.float32) * inv_freq
            cos = jnp.repeat(jnp.cos(angles), 2, axis=-1)
            sin = jnp.repeat(jnp.sin(angles), 2, axis=-1)
            x_rot = jnp.stack([-x[..., 1::2], x[..., 0::2]], axis=-1).reshape(x.shape)
            return x * cos + x_rot * sin
        b, s, _ = x.shape
        h, dk = (N_HEADS, D_K)
        proj = lambda W: jnp.einsum('bsi,oi->bso', x, W).reshape(b, s, h, dk).transpose(0, 2, 1, 3)
        q = proj(Wq)
        k = proj(Wk)
        v = proj(Wv)
        pos = jnp.arange(s)
        inv_freq = 1.0 / THETA ** (jnp.arange(0, dk, 2, dtype=jnp.float32) / dk)
        q = _rope(q, pos, inv_freq)
        k = _rope(k, pos, inv_freq)
        scores = jnp.einsum('bhqd,bhkd->bhqk', q, k) / jnp.sqrt(jnp.asarray(dk, jnp.float32))
        causal_mask = jnp.arange(s)[None, :] > jnp.arange(s)[:, None]
        scores = jnp.where(causal_mask, -jnp.inf, scores)
        weights = jax.nn.softmax(scores, axis=-1)
        out = jnp.einsum('bhqk,bhkd->bhqd', weights, v)
        out = out.transpose(0, 2, 1, 3).reshape(b, s, h * dk)
        return jnp.einsum('bsi,oi->bso', out, Wo)

    def _L1_ffn_ref(x, rw, rb, w1, b1, w2, b2, sw1, sb1, sw2, sb2):
        import jax, jax.numpy as jnp
        import numpy as np
        B, T, H, F, E, TOPK = (4, 256, 256, 1024, 8, 2)

        def _moe_forward(x, rw, rb, w1, b1, w2, b2, sw1, sb1, sw2, sb2):
            Bb, Tt, Hh = x.shape
            N = Bb * Tt
            Ee = rw.shape[0]
            cap = max(1, int(N / Ee * 1.0))
            xf = x.reshape(N, Hh)
            logits = xf @ rw.T + rb
            g_soft = jax.nn.softmax(logits, axis=-1)
            _, idx = jax.lax.top_k(g_soft, TOPK)
            primary, second = (idx[:, 0], idx[:, 1])
            ohp = jax.nn.one_hot(primary, Ee, dtype=jnp.int32)
            posp = jnp.cumsum(ohp, axis=0) - ohp
            pos_tok = jnp.take_along_axis(posp, primary[:, None], 1)[:, 0]
            keep_primary = pos_tok < cap
            used = jnp.minimum(ohp.sum(axis=0), cap)
            overflow = ~keep_primary
            ohs = jax.nn.one_hot(second, Ee, dtype=jnp.int32) * overflow[:, None].astype(jnp.int32)
            poss = jnp.cumsum(ohs, axis=0) - ohs
            pos2 = jnp.take_along_axis(poss, second[:, None], 1)[:, 0]
            take2 = overflow & (used[second] + pos2 < cap)
            assign = jnp.where(keep_primary, primary, jnp.where(take2, second, -1))
            overflow = overflow & ~take2
            h = jax.nn.gelu(jnp.einsum('nh,ehf->enf', xf, w1) + b1[:, None, :], approximate=False)
            stack = jnp.einsum('enf,efh->enh', h, w2) + b2[:, None, :]
            one_hot_a = jax.nn.one_hot(assign, Ee, dtype=stack.dtype)
            y = jnp.einsum('enh,ne->nh', stack, one_hot_a)
            y_fb = jax.nn.gelu(xf @ sw1 + sb1, approximate=False) @ sw2 + sb2
            y = jnp.where(overflow[:, None], y_fb, y)
            return y.reshape(Bb, Tt, Hh)
        return _moe_forward(x, rw, rb, w1, b1, w2, b2, sw1, sb1, sw2, sb2)
    h = _L0_tok_ref(L0_tok_log_dt, L0_tok_inv_A_real, L0_tok_A_imag, L0_tok_B_ri, x, 256)
    h = h + _L0_attn_ref(_layernorm(h, axis=-1), L0_attn_W_in, L0_attn_conv_w, L0_attn_ln_gamma, L0_attn_ln_beta, L0_attn_W_xproj, L0_attn_A_param, L0_attn_D, L0_attn_W_out)
    h = h + _L0_ffn_ref(_layernorm(h, axis=-1), L0_ffn_switch_w, L0_ffn_switch_b, L0_ffn_w1, L0_ffn_b1, L0_ffn_w2, L0_ffn_b2)
    h = h + _L1_attn_ref(_layernorm(h, axis=-1), L1_attn_Wq, L1_attn_Wk, L1_attn_Wv, L1_attn_Wo)
    h = h + _L1_ffn_ref(_layernorm(h, axis=-1), L1_ffn_rw, L1_ffn_rb, L1_ffn_w1, L1_ffn_b1, L1_ffn_w2, L1_ffn_b2, L1_ffn_sw1, L1_ffn_sb1, L1_ffn_sw2, L1_ffn_sb2)
    return h

_drawn_inputs = setup_inputs


def setup_inputs(seed=0):
    import zlib

    import numpy as np

    out = dict(_drawn_inputs(seed))
    spreads = {'L0_attn_ln_gamma': (1.0, 0.2),
     'L0_attn_ln_beta': (0.0, 0.1),
     'L0_attn_D': (1.0, 0.573),
     'L0_ffn_switch_b': (0.0, 0.49),
     'L0_ffn_b1': (0.0, 0.8),
     'L0_ffn_b2': (0.0, 0.8),
     'L1_ffn_rb': (0.0, 0.31),
     'L1_ffn_b1': (0.0, 0.8),
     'L1_ffn_b2': (0.0, 0.383),
     'L1_ffn_sb1': (0.0, 0.8),
     'L1_ffn_sb2': (0.0, 0.8)}
    factors = {'L0_attn_A_param': 4.128, 'L1_ffn_sw1': 8.0, 'L1_ffn_sw2': 7.738, 'L1_ffn_w1': 3.891}
    for name, (base, spread) in spreads.items():
        noise = np.random.default_rng([zlib.crc32(name.encode()), seed]).standard_normal(out[name].shape)
        drawn = base * np.exp(spread * noise) if base else spread * noise
        out[name] = jnp.asarray(drawn.astype(out[name].dtype))
    for name, factor in factors.items():
        out[name] = (out[name] * factor).astype(out[name].dtype)
    return out
```

```python
import math
from contextlib import ExitStack

import numpy as np

import concourse.bass as bass
from concourse import mybir

FP32 = mybir.dt.float32
BF16 = mybir.dt.bfloat16
I32 = mybir.dt.int32
U32 = mybir.dt.uint32
ALU = mybir.AluOpType
ACT = mybir.ActivationFunctionType
AX = mybir.AxisListType

P = 128
NB = 8
SEQ = 256
DM = 256
NS = 64
NTOK = NB * SEQ
NT = NTOK // P
TPB = SEQ // P
DC = DM // P
DI = 512
IC = DI // P
NA = 16
XP = 2 * NA + 1
KW = 4
FF = 1024
FC = FF // P
NE = 8
NH = 16
DK = DM // NH
EPS = 1e-5
CAP = NTOK // NE
LN2_HI = 0.693359375
LN2_LO = math.log(2) - LN2_HI
LOG_FLOOR = math.log(1e-6)


def memory(nc, ctx, stage):
    sb = lambda name, shape, dt=FP32: ctx.enter_context(nc.sbuf_tensor(f"{stage}_{name}", shape, dt))
    ps = lambda name, shape, dt=FP32: ctx.enter_context(nc.psum_tensor(f"{stage}_{name}", shape, dt))
    sem = lambda name: ctx.enter_context(nc.semaphore(f"{stage}_{name}"))
    return sb, ps, sem


def counting(base=0):
    n = [base]

    def one():
        n[0] += 1
        return 1

    return one, lambda: n[0]


def upto(item, per=1, k=None):
    return item * per + (2 * per + (per if k is None else k))


def spread(ap, dim, n):
    a = ap.unsqueeze(dim)
    shape = list(a.shape)
    shape[dim] = n
    return a.broadcast_to(shape)


def pipelined(eng, items, front, back):
    front(0, 0, 0)
    with eng.Fori(0, (items - 1) // 2) as i:
        front(2 * i + 1, 1, i)
        back(2 * i, 0, i)
        front(2 * i + 2, 0, i + 1)
        back(2 * i + 1, 1, i)
    last = items - 1
    if items % 2 == 0:
        front(last, 1, last // 2)
        back(last - 1, 0, last // 2)
    back(last, last % 2, last // 2)


def pipelined3(eng, items, front, back, late, late_first=False):
    def three(t, par, turn, more=True):
        if late_first:
            late(t, par, turn)
        if more:
            front(t + 2, par, turn + 1)
        back(t + 1, 1 - par, turn + par)
        if not late_first:
            late(t, par, turn)

    front(0, 0, 0)
    front(1, 1, 0)
    back(0, 0, 0)
    with eng.Fori(0, (items - 2) // 2) as i:
        three(2 * i, 0, i)
        three(2 * i + 1, 1, i)
    if items % 2:
        three(items - 3, 0, (items - 3) // 2)
    three(items - 2, items % 2, (items - 2) // 2, more=False)
    late(items - 1, (items - 1) % 2, (items - 1) // 2)


def nothing(item, par, turn):
    pass


def constants(nc, C, ident, ident_h, strict, ones):
    sb, ps, sem = memory(nc, C, "const")
    made = sem("made")
    with nc.Block() as block:

        @block.gpsimd
        def _(pool):
            one, total = counting()
            nc.gpsimd.memset(ident[:], 0.0).then_inc(made, one())
            nc.gpsimd.memset(ones[:], 1.0).then_inc(made, one())
            pool.wait_ge(made, total())
            nc.gpsimd.affine_select(out=ident[:], in_=ident[:], compare_op=ALU.not_equal, fill=1.0,
                                          base=0, pattern=[[-1, P]], channel_multiplier=1).then_inc(made, one())
            pool.wait_ge(made, total())
            nc.gpsimd.tensor_copy(ident_h[:], ident[:]).then_inc(made, one())
            nc.gpsimd.affine_select(out=strict[:], in_=ones[:], compare_op=ALU.is_gt, fill=0.0,
                                          base=0, pattern=[[1, P]], channel_multiplier=-1).then_inc(made, one())
            pool.wait_ge(made, total())


NG = SEQ // 2
NLO = 32
NHI = DM // NLO
CB = NB * NHI


def s4_kernel(nc, h, ident, log_dt, inv_a, a_imag, b_ri, x):
    with ExitStack() as ctx:
        sb, ps, sem = memory(nc, ctx, "s4")
        d_re = sb("d_re", [P, 8, NG])
        d_im = sb("d_im", [P, 8, NG])
        c_re = sb("c_re", [P, NB, NG])
        c_im = sb("c_im", [P, NB, NG])
        v_re = sb("v_re", [P, NG, NLO])
        v_im = sb("v_im", [P, NG, NLO])
        w_re = sb("w_re", [P, NG, NHI])
        w_im = sb("w_im", [P, NG, NHI])
        half = sb("half", [P, 2, 2])
        with ExitStack() as ctx2:
            sb, ps, sem = memory(nc, ctx2, "s4a")
            logs = sb("logs", [NG, 2 + P])
            exps = sb("exps", [NG, 2 + P])
            frac = sb("frac", [NG, 2 + P])
            whole = sb("whole", [NG, 2 + P])
            whole_i = sb("whole_i", [NG, 2 + P], I32)
            dt2, ar = exps[:, 0:2], exps[:, 2:]
            im = sb("im", [NG, P])
            bt = sb("bt", [NG, P, 2])
            xt = sb("xt", [NG, NB, P, 2])
            da = sb("da", [NG, 2, P])
            tm = sb("tm", [NG, 6, P])
            cr = sb("cr", [NG, NB, P])
            ci = sb("ci", [NG, NB, P])
            c1 = sb("c1", [NG, NB, P])
            c2 = sb("c2", [NG, NB, P])
            loaded = [sem(f"loaded{i}") for i in range(2)]
            made = sem("made")
            masked = sem("masked")
            turned = sem("turned")
            da_ready = sem("da_ready")
            c_ready = sem("c_ready")
            moved = sem("moved")
            t_ps = ps("t_ps", [P, 2 + 2 * NB, P])
            s1 = sb("s1", [P, NG, NLO // 2])
            t2 = sb("t2", [P, NG, NLO // 2])
            s3 = sb("s3", [P, NG, NHI // 2])
            t4 = sb("t4", [P, NG, NHI // 2])
            squared = sem("squared")

            def double(eng, e, made, one, total, a, b, re, im_, m, k):
                dr, di = spread(d_re[:, k, :], 2, m), spread(d_im[:, k, :], 2, m)
                a, b = a[:, :, 0:m], b[:, :, 0:m]
                new_r, new_i = re[:, :, m:2 * m], im_[:, :, m:2 * m]
                e.tensor_tensor(a, re[:, :, 0:m], dr, ALU.mult).then_inc(made, one())
                e.tensor_tensor(b, im_[:, :, 0:m], di, ALU.mult).then_inc(made, one())
                e.tensor_tensor(new_i, re[:, :, 0:m], di, ALU.mult).then_inc(made, one())
                eng.wait_ge(made, total())
                e.tensor_tensor(new_r, a, b, ALU.subtract).then_inc(made, one())
                eng.wait_ge(made, total())
                e.tensor_tensor(a, im_[:, :, 0:m], dr, ALU.mult).then_inc(made, one())
                eng.wait_ge(made, total())
                e.tensor_tensor(new_i, new_i, a, ALU.add).then_inc(made, one())
                eng.wait_ge(made, total())

            with nc.Block() as block:

                @block.sync
                def _(sp):
                    sp.dma_start(logs[:, 0:2], log_dt.rearrange("(g k) -> g k", k=2)).then_inc(loaded[0], 16)
                    sp.dma_start(logs[:, 2:], inv_a.rearrange("(g k) n -> g (k n)", k=2)).then_inc(loaded[0], 16)
                    sp.dma_start(im[:], a_imag.rearrange("(g k) n -> g (k n)", k=2)).then_inc(loaded[0], 16)
                    sp.dma_start(bt[:], b_ri.rearrange("(g k) n r -> g (k n) r", k=2)).then_inc(loaded[1], 16)
                    sp.dma_start(xt[:], x.rearrange("c (g k) n r -> g c (k n) r", k=2)).then_inc(loaded[1], 16)

                @block.scalar
                def _(act):
                    act.wait_ge(turned, 2)
                    nc.scalar.copy(c_re[:], t_ps[:, 2:2 + NB, :]).then_inc(moved, 1)
                    nc.scalar.copy(c_im[:], t_ps[:, 2 + NB:2 + 2 * NB, :]).then_inc(moved, 1)

                @block.gpsimd
                def _(pool):
                    nc.gpsimd.memset(half[:], 0.0).then_inc(masked, 1)
                    pool.wait_ge(masked, 1)
                    for k in range(2):
                        for r, sign in enumerate((1.0, -1.0)):
                            nc.gpsimd.memset(half[k * NS:(k + 1) * NS, k, r:r + 1], sign).then_inc(masked, 1)
                    one, total = counting(5)
                    pool.wait_ge(masked, total())
                    nc.gpsimd.memset(w_re[:, :, 0:1], 1.0).then_inc(masked, one())
                    pool.wait_ge(masked, total())
                    nc.gpsimd.memset(w_im[:, :, 0:1], 0.0).then_inc(masked, one())
                    pool.wait_ge(masked, total())
                    pool.wait_ge(squared, 1)
                    for k in range(3):
                        double(pool, nc.gpsimd, masked, one, total, s3, t4, w_re, w_im, 1 << k, 5 + k)

                @block.tensor
                def _(pe):
                    pe.wait_ge(da_ready, 2)
                    for r in range(2):
                        last = nc.tensor.transpose(t_ps[:, r, :], da[:, r, :], ident[:])
                    last.then_inc(turned, 1)
                    pe.wait_ge(c_ready, 2)
                    for c in range(NB):
                        nc.tensor.transpose(t_ps[:, 2 + c, :], cr[:, c, :], ident[:])
                        last = nc.tensor.transpose(t_ps[:, 2 + NB + c, :], ci[:, c, :], ident[:])
                    last.then_inc(turned, 1)

                @block.vector
                def _(dve):
                    v = nc.vector
                    one, total = counting()
                    by_k = lambda a: a.rearrange("g (k n) -> g k n", k=2)
                    dve.wait_ge(loaded[0], 48)
                    v.tensor_scalar(logs[:], logs[:], -87.0, 88.0, op0=ALU.max, op1=ALU.min).then_inc(made, one())
                    dve.wait_ge(made, total())
                    v.tensor_scalar(whole_i[:], logs[:], 1 / math.log(2), None, op0=ALU.mult).then_inc(made, one())
                    dve.wait_ge(made, total())
                    v.tensor_copy(whole[:], whole_i[:]).then_inc(made, one())
                    dve.wait_ge(made, total())
                    v.scalar_tensor_tensor(frac[:], whole[:], -LN2_HI, logs[:], op0=ALU.mult, op1=ALU.add).then_inc(made, one())
                    dve.wait_ge(made, total())
                    v.scalar_tensor_tensor(frac[:], whole[:], -LN2_LO, frac[:], op0=ALU.mult, op1=ALU.add).then_inc(made, one())
                    dve.wait_ge(made, total())
                    v.tensor_scalar(whole_i[:], whole[:], 127.0, 2.0 ** 23, op0=ALU.add, op1=ALU.mult).then_inc(made, one())
                    v.tensor_scalar(exps[:], frac[:], 1 / math.factorial(10), None, op0=ALU.mult).then_inc(made, one())
                    dve.wait_ge(made, total())
                    for k in range(9, 0, -1):
                        v.scalar_tensor_tensor(exps[:], exps[:], 1 / math.factorial(k), frac[:],
                                                     op0=ALU.add, op1=ALU.mult).then_inc(made, one())
                        dve.wait_ge(made, total())
                    v.scalar_tensor_tensor(exps[:], exps[:], 1.0, whole_i[:].bitcast(FP32), op0=ALU.add,
                                                 op1=ALU.mult).then_inc(made, one())
                    dve.wait_ge(made, total())
                    v.tensor_scalar(dt2, dt2, 0.5, None, op0=ALU.mult).then_inc(made, one())
                    dve.wait_ge(made, total())
                    v.tensor_tensor(by_k(tm[:, 0, :]), by_k(ar), spread(dt2, 2, NS), ALU.mult).then_inc(made, one())
                    v.tensor_tensor(by_k(tm[:, 1, :]), by_k(im[:]), spread(dt2, 2, NS), ALU.mult).then_inc(made, one())
                    dve.wait_ge(made, total())
                    v.tensor_tensor(tm[:, 2, :], tm[:, 0, :], tm[:, 0, :], ALU.mult).then_inc(made, one())
                    v.tensor_tensor(tm[:, 3, :], tm[:, 1, :], tm[:, 1, :], ALU.mult).then_inc(made, one())
                    v.tensor_scalar(tm[:, 4, :], tm[:, 0, :], 1.0, None, op0=ALU.add).then_inc(made, one())
                    dve.wait_ge(made, total())
                    v.tensor_tensor(tm[:, 5, :], tm[:, 4, :], tm[:, 4, :], ALU.mult).then_inc(made, one())
                    dve.wait_ge(made, total())
                    v.tensor_tensor(tm[:, 5, :], tm[:, 5, :], tm[:, 3, :], ALU.add).then_inc(made, one())
                    v.tensor_tensor(tm[:, 2, :], tm[:, 2, :], tm[:, 3, :], ALU.add).then_inc(made, one())
                    dve.wait_ge(made, total())
                    v.tensor_scalar(tm[:, 2, :], tm[:, 2, :], -1.0, 1.0, op0=ALU.mult, op1=ALU.add).then_inc(made, one())
                    v.reciprocal(tm[:, 5, :], tm[:, 5, :]).then_inc(made, one())
                    dve.wait_ge(made, total())
                    v.tensor_tensor(da[:, 0, :], tm[:, 2, :], tm[:, 5, :], ALU.mult).then_inc(da_ready, 1)
                    v.scalar_tensor_tensor(da[:, 1, :], tm[:, 1, :], 2.0, tm[:, 5, :], op0=ALU.mult,
                                           op1=ALU.mult).then_inc(da_ready, 1)
                    dve.wait_ge(loaded[1], 32)
                    xr, xi = xt[:, :, :, 0], xt[:, :, :, 1]
                    br, bi = spread(bt[:, :, 0], 1, NB), spread(bt[:, :, 1], 1, NB)
                    v.scalar_tensor_tensor(c1[:], xr, 2.0, br, op0=ALU.mult, op1=ALU.mult).then_inc(made, one())
                    v.scalar_tensor_tensor(c2[:], xi, 2.0, bi, op0=ALU.mult, op1=ALU.mult).then_inc(made, one())
                    v.scalar_tensor_tensor(cr[:], xr, 2.0, bi, op0=ALU.mult, op1=ALU.mult).then_inc(made, one())
                    v.scalar_tensor_tensor(ci[:], xi, 2.0, br, op0=ALU.mult, op1=ALU.mult).then_inc(made, one())
                    dve.wait_ge(made, total())
                    v.tensor_tensor(ci[:], ci[:], cr[:], ALU.add).then_inc(made, one())
                    dve.wait_ge(made, total())
                    v.tensor_tensor(cr[:], c1[:], c2[:], ALU.subtract).then_inc(c_ready, 1)
                    dve.wait_ge(turned, 1)
                    v.tensor_copy(d_re[:, 0, :], t_ps[:, 0, :]).then_inc(made, one())
                    v.tensor_copy(d_im[:, 0, :], t_ps[:, 1, :]).then_inc(c_ready, 1)
                    v.memset(v_re[:, :, 0:1], 1.0).then_inc(made, one())
                    v.memset(v_im[:, :, 0:1], 0.0).then_inc(made, one())
                    dve.wait_ge(made, total())
                    dve.wait_ge(c_ready, 2)

                    def square(k):
                        a, b = s1[:, :, 0], t2[:, :, 0]
                        r, i = d_re[:, k, :], d_im[:, k, :]
                        v.tensor_tensor(a, r, r, ALU.mult).then_inc(made, one())
                        v.tensor_tensor(b, i, i, ALU.mult).then_inc(made, one())
                        v.scalar_tensor_tensor(d_im[:, k + 1, :], r, 2.0, i, op0=ALU.mult, op1=ALU.mult).then_inc(made, one())
                        dve.wait_ge(made, total())
                        v.tensor_tensor(d_re[:, k + 1, :], a, b, ALU.subtract).then_inc(made, one())
                        dve.wait_ge(made, total())

                    for k in range(7):
                        square(k)
                    dve.sem_inc(squared, 1)
                    for k in range(5):
                        double(dve, v, made, one, total, s1, t2, v_re, v_im, 1 << k, k)

        with ExitStack() as ctx3:
            sb, ps, sem = memory(nc, ctx3, "s4b")
            GC = 16
            NQ = NG // 2 // GC
            cw = sb("cw", [P, 2, 4, GC, CB])
            vd = sb("vd", [P, 2, 3, GC, 2, NLO])
            k_sb = sb("k_sb", [P, NG, NLO])
            prod = [ps(f"prod{i}", [P, GC, 2 * NLO]) for i in range(2)]
            t_ps = ps("t_ps", [P, 4, 4, P])
            cw_ready, vd_ready, mm_done, k_ready = (sem(n) for n in ("cw_ready", "vd_ready", "mm_done", "k_ready"))
            turned, t_free = sem("turned"), [sem(f"t_free{i}") for i in range(2)]
            LEAD = 2

            def unpack(eng, copy, first):
                hv = h[:].rearrange("p (c f) (b a) -> p f c b a", f=2, b=NHI)
                for n in range(first, NLO // 4, 2):
                    eng.wait_ge(turned, n + 1)
                    src = t_ps[:, n % 4].rearrange("p a (f c b) -> p f c b a", f=2, c=NB)
                    for f in range(2):
                        copy(hv[:, f, :, :, 4 * n:4 * n + 4], src[:, f]).then_inc(t_free[first], 1)

            with nc.Block() as block:

                @block.vector
                def _(dve):
                    with dve.Fori(0, NQ) as q:
                        for hf in range(2):
                            dve.wait_ge(mm_done, 2 * q + hf + 1)
                            g = q * GC + hf * (NG // 2)
                            for k, (c, w) in enumerate(((c_re, w_re), (c_im, w_im), (c_re, w_im), (c_im, w_re))):
                                o = cw[:, hf, k].rearrange("p g (c b) -> p g c b", c=NB)
                                a = spread(c[:, :, bass.ds(g, GC)].rearrange("p c g -> p g c"), 3, NHI)
                                b = spread(w[:, bass.ds(g, GC), :], 2, NB)
                                nc.vector.tensor_tensor(o, a, b, ALU.mult).then_inc(cw_ready, 1)
                    unpack(dve, nc.vector.tensor_copy, 0)

                @block.scalar
                def _(act):
                    def front(t, hf, q):
                        act.wait_ge(mm_done, t + 1)
                        g = q * GC + hf * (NG // 2)
                        for k, (vt, neg) in enumerate(((v_re, 0), (v_re, 1), (v_im, 1))):
                            for ch in range(2):
                                nc.scalar.activation(vd[:, hf, k, :, ch, :], vt[:, bass.ds(g, GC), :], ACT.Copy,
                                                     scale=half[:, ch, neg:neg + 1]).then_inc(vd_ready, 1)

                    def back(t, hf, q):
                        act.wait_ge(mm_done, t + 1 + LEAD)
                        rows = slice(hf * CB, (hf + 1) * CB)
                        nc.scalar.copy(k_sb[rows, bass.ds(2 * GC * q, 2 * GC), :],
                                       prod[hf][rows].rearrange("r g (k a) -> r (g k) a", k=2)).then_inc(k_ready, 1)

                    pipelined(act, 2 * NQ, front, back)
                    unpack(act, nc.scalar.copy, 1)

                @block.tensor
                def _(pe):
                    pe.sem_inc(mm_done, LEAD)
                    with pe.Fori(0, NQ) as q:
                        for hf in range(2):
                            pe.wait_ge(cw_ready, 8 * q + 4 * hf + 4)
                            pe.wait_ge(vd_ready, 12 * q + 6 * hf + 6)
                            rows = slice(hf * CB, (hf + 1) * CB)
                            for g in range(GC):
                                for k, m in enumerate((0, 1, 2, 2)):
                                    last = nc.tensor.matmul(prod[hf][rows, g, :], cw[:, hf, k, g, :],
                                                            vd[:, hf, m, g].rearrange("p k a -> p (k a)"),
                                                            start=k == 0, stop=k == 3)
                            last.then_inc(mm_done, 1)
                    pe.wait_ge(k_ready, 2 * NQ)
                    for n in range(NLO // 4):
                        if n >= 4:
                            pe.wait_ge(t_free[n % 2], 2 * (n // 2 - 1))
                        for i in range(4):
                            last = nc.tensor.transpose(t_ps[:, n % 4, i, :], k_sb[:, :, 4 * n + i], ident[:])
                        last.then_inc(turned, 1)


def tile_of(ap, t):
    return ap[:, bass.ds(t, 1)].rearrange("p a b -> p (a b)")


def stats_tables(nc, ctx, stage):
    sb, ps, sem = memory(nc, ctx, stage)
    six = sb("six", [P, NT, 6])
    tables = [sb(n, [P, NT]) for n in ("sum_", "diff", "var", "root", "mean", "rstd")]
    return six, tables, sem("var_ready"), sem("root_ready")


def stats_root(nc, act, stats):
    six, (_, _, var, root, _, _), var_ready, root_ready = stats
    act.wait_ge(var_ready, 1)
    nc.scalar.activation(root[:], var[:], ACT.Sqrt).then_inc(root_ready, 1)


def stats_finish(nc, dve, stats, width, made, one, total):
    six, (a, b, var, root, mean, r), var_ready, root_ready = stats
    v = nc.vector
    v.tensor_tensor(a[:], six[:, :, 1], six[:, :, 4], ALU.add).then_inc(made, one())
    v.tensor_tensor(b[:], six[:, :, 1], six[:, :, 4], ALU.subtract).then_inc(made, one())
    v.tensor_tensor(var[:], six[:, :, 2], six[:, :, 5], ALU.add).then_inc(made, one())
    dve.wait_ge(made, total())
    v.tensor_scalar(mean[:], a[:], 0.5, None, op0=ALU.mult).then_inc(made, one())
    v.tensor_scalar(var[:], var[:], 1.0 / width, EPS, op0=ALU.mult, op1=ALU.add).then_inc(made, one())
    v.scalar_tensor_tensor(b[:], b[:], 0.25, b[:], op0=ALU.mult, op1=ALU.mult).then_inc(made, one())
    dve.wait_ge(made, total())
    v.tensor_tensor(var[:], var[:], b[:], ALU.add).then_inc(var_ready, 1)
    dve.wait_ge(root_ready, 1)
    v.reciprocal(r[:], root[:]).then_inc(made, one())
    dve.wait_ge(made, total())
    v.tensor_tensor(a[:], r[:], r[:], ALU.mult).then_inc(made, one())
    dve.wait_ge(made, total())
    v.tensor_tensor(a[:], a[:], var[:], ALU.mult).then_inc(made, one())
    dve.wait_ge(made, total())
    v.tensor_scalar(a[:], a[:], -0.5, 1.5, op0=ALU.mult, op1=ALU.add).then_inc(made, one())
    dve.wait_ge(made, total())
    v.tensor_tensor(r[:], r[:], a[:], ALU.mult).then_inc(made, one())
    dve.wait_ge(made, total())


def row_stats(nc, ctx, stage, h):
    stats = stats_tables(nc, ctx, stage)
    six, (_, _, _, _, mean, rstd), _, _ = stats
    sb, ps, sem = memory(nc, ctx, stage)
    made = sem("stats_made")
    with nc.Block() as block:

        @block.vector
        def _(dve):
            with dve.Fori(0, NT // 8) as i:
                for t in range(8):
                    nc.vector.bn_stats(tile_of(six, 8 * i + t), tile_of(h, 8 * i + t)).then_inc(made, 1)
            one, total = counting(NT)
            dve.wait_ge(made, total())
            stats_finish(nc, dve, stats, DM, made, one, total)

        @block.scalar
        def _(act):
            stats_root(nc, act, stats)

    return mean, rstd


def gated_layer(nc, h, ident, w_in, conv_w, gamma, beta, gamma_col, beta_col, w_x, a_param, d_param, w_out, a_neg):
    PE_N = 11
    with ExitStack() as ctx:
        sb, ps, sem = memory(nc, ctx, "gate")
        xc = sb("xc", [P, NT, DI])
        sz = sb("sz", [P, NT, DI])
        ab = sb("ab", [P, NA * DI])
        g_row = sb("g_row", [P, DI])
        b_row = sb("b_row", [P, DI])
        d_row = sb("d_row", [P, DI])
        wo = sb("wo", [P, IC, DM])
        delta = sb("delta", [P, NT])
        bc = sb("bc", [P, NT, NA])
        inner = stats_tables(nc, ctx, "gate_in")
        in_six, (_, _, _, _, in_mean, in_rstd), _, _ = inner
        small_loaded, rows_loaded, a_stored, a_loaded = (
            sem(n) for n in ("small_loaded", "rows_loaded", "a_stored", "a_loaded"))
        a_steps, a_made, wx_made, sums_made = sem("a_steps"), sem("a_made"), sem("wx_made"), sem("sums_made")
        products = ctx.enter_context(ExitStack())
        sb, ps, sem = memory(nc, products, "gate_products")
        raw = sb("raw", [P, NT, XP])
        c1c0 = sb("c1c0", [P, 2, XP])
        with ExitStack() as ctx2:
            sb, ps, sem = memory(nc, ctx2, "gatea")
            wi = sb("wi", [P, DC, 2 * DI])
            wx = sb("wx", [P, IC, XP])
            gwx = sb("gwx", [P, IC, XP])
            taps = sb("taps", [P, IC, KW])
            gb = sb("gb", [P, 2, IC])
            gbs = sb("gbs", [P, 2, IC, P])
            ones = sb("ones", [P, P])
            ap_ = sb("ap", [P, DI * NA // P])
            t1 = sb("t1", [P, DI * NA // P])
            xn = sb("xn", [P, 2, TPB, DM])
            xt = sb("xt", [P, 2, DC, SEQ])
            xpad = sb("xpad", [P, 2, IC, KW - 1 + SEQ])
            acc = sb("acc", [P, 2, IC, SEQ])
            xcf = sb("xcf", [P, 2, IC, SEQ])
            t_ps = ps("t_ps", [P, DC, SEQ])
            x_ps = ps("x_ps", [P, IC, SEQ])
            z_ps = ps("z_ps", [P, TPB, DI])
            y_ps = ps("y_ps", [P, TPB, DI])
            r_ps = ps("r_ps", [P, TPB, 64])
            mean, rstd = row_stats(nc, ctx2, "ln0", h)
            w1_sem = sem("w1")
            chain = sem("chain")
            ones_made = sem("ones_made")
            xn_ready = sem("xn_ready")
            x_turned = sem("x_turned")
            xt_ready = sem("xt_ready")
            xc_done = sem("xc_done")
            xc_moved = sem("xc_moved")
            z_done = sem("z_done")
            z_ready = sem("z_ready")
            conv = sem("conv")
            act_ready = sem("act_ready")
            raw_done = sem("raw_done")
            raw_moved = sem("raw_moved")
            y_turned = sem("y_turned")
            y_moved = sem("y_moved")
            stats_done = sem("stats_done")
            with nc.Block() as block:

                @block.sync
                def _(sp):
                    sp.dma_start(wi[:], w_in.rearrange("(c p) n -> p c n", p=P)).then_inc(w1_sem, 16)
                    sp.dma_start(ap_[:], a_param).then_inc(small_loaded, 16)
                    sp.dma_start(wx[:], w_x.rearrange("(c p) n -> p c n", p=P)).then_inc(small_loaded, 16)
                    sp.dma_start(taps[:], conv_w.rearrange("(c p) o k -> p c (o k)", p=P)).then_inc(small_loaded, 16)
                    sp.dma_start(gb[:, 0, :], gamma_col).then_inc(small_loaded, 16)
                    sp.dma_start(gb[:, 1, :], beta_col).then_inc(small_loaded, 16)
                    for row, src in ((g_row, gamma), (b_row, beta), (d_row, d_param)):
                        sp.dma_start(row[:], src.partition_broadcast(P)).then_inc(rows_loaded, 16)
                    sp.dma_start(wo[:], w_out.rearrange("(c p) n -> p c n", p=P)).then_inc(rows_loaded, 16)
                    sp.wait_ge(a_made, 1)
                    sp.dma_start(a_neg.rearrange("(p c) -> p c", p=P), ap_[:]).then_inc(a_stored, 16)
                    sp.wait_ge(a_stored, 16)
                    sp.dma_start(ab[:], a_neg.partition_broadcast(P)).then_inc(a_loaded, 16)

                @block.gpsimd
                def _(pool):
                    nc.gpsimd.memset(ones[:], 1.0).then_inc(ones_made, 1)
                    for par in range(2):
                        nc.gpsimd.memset(xpad[:, par, :, 0:KW - 1], 0.0).then_inc(ones_made, 1)
                    pool.wait_ge(small_loaded, 80)
                    pool.wait_ge(ones_made, 1)
                    for k in range(2):
                        nc.gpsimd.tensor_copy(gbs[:, k], spread(gb[:, k, :], 2, P)).then_inc(ones_made, 1)

                @block.scalar
                def _(act):
                    for signal, per in ((xt_ready, 1), (xc_moved, 2), (z_ready, TPB), (act_ready, 1), (y_moved, TPB)):
                        act.sem_inc(signal, 2 * per)
                    act.wait_ge(small_loaded, 80)
                    nc.scalar.activation(t1[:], ap_[:], ACT.Abs).then_inc(a_steps, 1)
                    act.wait_ge(a_steps, 1)
                    nc.scalar.activation(t1[:], t1[:], ACT.Exp, scale=-1.0).then_inc(a_steps, 1)
                    act.wait_ge(a_steps, 2)
                    nc.scalar.activation(t1[:], t1[:], ACT.Ln, bias=1.0).then_inc(a_steps, 1)

                    def front(b, par, turn):
                        act.wait_ge(x_turned, upto(b))
                        act.wait_ge(xc_done, upto(b - 2))
                        act.wait_ge(z_done, upto(b - 2, TPB))
                        nc.scalar.copy(xt[:, par], t_ps[:]).then_inc(xt_ready, 1)
                        act.wait_ge(xc_done, upto(b))
                        act.wait_ge(conv, upto(b - 2, IC * KW))
                        for k in range(2):
                            nc.scalar.copy(xpad[:, par, 2 * k:2 * k + 2, KW - 1:],
                                                           x_ps[:, 2 * k:2 * k + 2]).then_inc(xc_moved, 1)

                    def back(b, par, turn):
                        act.wait_ge(conv, upto(b, IC * KW))
                        act.wait_ge(raw_done, upto(b - 2))
                        act.wait_ge(y_turned, upto(b - 2, TPB))
                        nc.scalar.activation(xcf[:, par], acc[:, par], ACT.Silu).then_inc(act_ready, 1)
                        for k in range(TPB):
                            act.wait_ge(z_done, upto(b, TPB, k + 1))
                            nc.scalar.activation(tile_of(sz, TPB * b + k), z_ps[:, k], ACT.Silu).then_inc(z_ready, 1)

                    def late(b, par, turn):
                        for k in range(TPB):
                            act.wait_ge(y_turned, upto(b, TPB, k + 1))
                            nc.scalar.copy(tile_of(xc, TPB * b + k), y_ps[:, k]).then_inc(y_moved, 1)

                    pipelined3(act, NB, front, back, late)

                @block.vector
                def _(dve):
                    v = nc.vector
                    for signal, per in ((xn_ready, TPB), (conv, IC * KW), (raw_moved, 1), (stats_done, TPB)):
                        dve.sem_inc(signal, 2 * per)
                    one, total = counting()
                    dve.wait_ge(a_steps, 3)
                    dve.wait_ge(small_loaded, 80)
                    v.scalar_tensor_tensor(ap_[:], ap_[:], 0.0, t1[:], op0=ALU.max, op1=ALU.add).then_inc(chain, one())
                    dve.wait_ge(chain, total())
                    v.tensor_scalar(ap_[:], ap_[:], 0.1, 10.0, op0=ALU.max, op1=ALU.min).then_inc(chain, one())
                    dve.wait_ge(chain, total())
                    v.tensor_scalar(ap_[:], ap_[:], -1.0, None, op0=ALU.mult).then_inc(a_made, 1)
                    for m in range(IC):
                        v.tensor_scalar(gwx[:, m], wx[:, m], gb[:, 0, m:m + 1], None, op0=ALU.mult).then_inc(wx_made, 1)
                    dve.wait_ge(sums_made, 1)
                    v.tensor_copy(c1c0[:], r_ps[:, :, 0:XP]).then_inc(wx_made, 1)
                    dve.wait_ge(wx_made, IC + 1)
                    dve.wait_ge(ones_made, 3)

                    def front(b, par, turn):
                        dve.wait_ge(x_turned, upto(b - 2))
                        for k in range(TPB):
                            t = TPB * b + k
                            v.tensor_scalar(xn[:, par, k], tile_of(h, t), mean[:, bass.ds(t, 1)],
                                                            rstd[:, bass.ds(t, 1)], op0=ALU.subtract, op1=ALU.mult).then_inc(xn_ready, 1)

                    def back(b, par, turn):
                        dve.wait_ge(act_ready, upto(b - 2))
                        dve.wait_ge(xc_moved, upto(b, 2))
                        for m in range(IC):
                            v.tensor_scalar(acc[:, par, m], xpad[:, par, m, KW - 1:], taps[:, m, KW - 1:KW],
                                                        None, op0=ALU.mult).then_inc(conv, 1)
                        for j in range(1, KW):
                            for m in range(IC):
                                dve.wait_ge(conv, upto(b, IC * KW, IC * (j - 1) + m + 1))
                                v.scalar_tensor_tensor(
                                    acc[:, par, m], xpad[:, par, m, KW - 1 - j:KW - 1 - j + SEQ],
                                    taps[:, m, KW - 1 - j:KW - j], acc[:, par, m], op0=ALU.mult, op1=ALU.add).then_inc(conv, 1)

                    def late(b, par, turn):
                        dve.wait_ge(raw_done, upto(b))
                        v.tensor_copy(raw[:, bass.ds(TPB * b, TPB)], r_ps[:, :, 0:XP]).then_inc(raw_moved, 1)
                        for k in range(TPB):
                            dve.wait_ge(y_moved, upto(b, TPB, k + 1))
                            t = TPB * b + k
                            v.bn_stats(tile_of(in_six, t), tile_of(xc, t)).then_inc(stats_done, 1)

                    pipelined3(dve, NB, front, back, late)

                @block.tensor
                def _(pe):
                    mm = nc.tensor.matmul
                    for signal, per in ((x_turned, 1), (xc_done, 1), (z_done, TPB), (raw_done, 1), (y_turned, TPB)):
                        pe.sem_inc(signal, 2 * per)
                    pe.wait_ge(small_loaded, 80)
                    pe.wait_ge(ones_made, 5)
                    for k in range(2):
                        for m in range(IC):
                            last = mm(r_ps[:, k, 0:XP], gbs[:, k, m], wx[:, m], start=m == 0, stop=m == IC - 1)
                    last.then_inc(sums_made, 1)
                    pe.wait_ge(wx_made, IC + 1)
                    pe.wait_ge(w1_sem, 16)

                    def front(b, par, turn):
                        pe.wait_ge(xn_ready, upto(b, TPB))
                        pe.wait_ge(xt_ready, upto(b - 1))
                        for k in range(TPB):
                            for c in range(DC):
                                last = nc.tensor.transpose(t_ps[:, c, k * P:(k + 1) * P],
                                                           xn[:, par, k, c * P:(c + 1) * P], ident[:])
                        last.then_inc(x_turned, 1)
                        pe.wait_ge(xt_ready, upto(b))
                        pe.wait_ge(xc_moved, upto(b - 1, 2))
                        for m in range(IC):
                            for c in range(DC):
                                last = mm(x_ps[:, m], wi[:, c, m * P:(m + 1) * P], xt[:, par, c],
                                          start=c == 0, stop=c == DC - 1)
                        last.then_inc(xc_done, 1)

                    def back(b, par, turn):
                        for k in range(TPB):
                            pe.wait_ge(z_ready, upto(b - 1, TPB, k + 1))
                            for c in range(DC):
                                last = mm(z_ps[:, k], xt[:, par, c, k * P:(k + 1) * P], wi[:, c, DI:2 * DI],
                                          start=c == 0, stop=c == DC - 1)
                            last.then_inc(z_done, 1)
                        pe.wait_ge(act_ready, upto(b))
                        pe.wait_ge(raw_moved, upto(b - 1))
                        for k in range(TPB):
                            for m in range(IC):
                                last = mm(r_ps[:, k, 0:XP], xcf[:, par, m, k * P:(k + 1) * P], gwx[:, m],
                                          start=m == 0, stop=m == IC - 1)
                        last.then_inc(raw_done, 1)
                        for k in range(TPB):
                            pe.wait_ge(y_moved, upto(b - 1, TPB, k + 1))
                            for m in range(IC):
                                last = nc.tensor.transpose(y_ps[:, k, m * P:(m + 1) * P],
                                                           xcf[:, par, m, k * P:(k + 1) * P], ident[:])
                            last.then_inc(y_turned, 1)

                    pipelined3(pe, NB, front, back, nothing)

        with ExitStack() as ctx3:
            sb, ps, sem = memory(nc, ctx3, "gateb")
            xp = sb("xp", [P, NT, XP])
            xq = sb("xq", [P, NT, XP])
            sp1 = sb("sp1", [P, NT])
            chain = sem("chain")
            xp_ready = sem("xp_ready")
            soft = sem("soft")
            with nc.Block() as block:

                @block.scalar
                def _(act):
                    stats_root(nc, act, inner)
                    act.wait_ge(xp_ready, 1)
                    nc.scalar.activation(sp1[:], xp[:, :, 0], ACT.Abs).then_inc(soft, 1)
                    act.wait_ge(soft, 1)
                    nc.scalar.activation(sp1[:], sp1[:], ACT.Exp, scale=-1.0).then_inc(soft, 1)
                    act.wait_ge(soft, 2)
                    nc.scalar.activation(sp1[:], sp1[:], ACT.Ln, bias=1.0).then_inc(soft, 1)

                @block.vector
                def _(dve):
                    v = nc.vector
                    one, total = counting()
                    stats_finish(nc, dve, inner, DI, chain, one, total)
                    c1, c0 = spread(c1c0[:, 0], 1, NT), spread(c1c0[:, 1], 1, NT)
                    v.tensor_tensor(xq[:], c1, spread(in_mean[:], 2, XP), ALU.mult).then_inc(chain, one())
                    dve.wait_ge(chain, total())
                    v.tensor_tensor(xp[:], raw[:], xq[:], ALU.subtract).then_inc(chain, one())
                    dve.wait_ge(chain, total())
                    v.tensor_tensor(xp[:], xp[:], spread(in_rstd[:], 2, XP), ALU.mult).then_inc(chain, one())
                    dve.wait_ge(chain, total())
                    v.tensor_tensor(xp[:], xp[:], c0, ALU.add).then_inc(xp_ready, 1)
                    dve.wait_ge(xp_ready, 1)
                    v.tensor_tensor(bc[:], xp[:, :, 1:1 + NA], xp[:, :, 1 + NA:], ALU.mult)
                    dve.wait_ge(soft, 3)
                    v.scalar_tensor_tensor(delta[:], xp[:, :, 0], 0.0, sp1[:], op0=ALU.max, op1=ALU.add).then_inc(chain, one())
                    dve.wait_ge(chain, total())
                    v.tensor_scalar(delta[:], delta[:], 1e-6, 10.0, op0=ALU.max, op1=ALU.min)

        products.close()
        with ExitStack() as ctx4:
            sb, ps, sem = memory(nc, ctx4, "gatec")
            e = sb("e", [P, 2, NA, DI])
            diag = sb("diag", [P, 2, PE_N, P])
            acc = sb("acc", [P, 2, DI])
            yt = sb("yt", [P, IC, P])
            s_ps = [ps(f"s_ps{i}", [P, DI]) for i in range(2)]
            y_ps = ps("y_ps", [P, IC, P])
            o_ps = ps("o_ps", [P, 512])
            NCH = 4
            PER = NA // NCH
            arg_ready = sem("arg_ready")
            e_ready = sem("e_ready")
            diag_ready = sem("diag_ready")
            sum_done = sem("sum_done")
            norm_ready = sem("norm_ready")
            xh_ready = sem("xh_ready")
            steps = sem("steps")
            y_turned = sem("y_turned")
            yt_ready = sem("yt_ready")
            o_done = sem("o_done")
            h_done = sem("h_done")
            apart = sem("apart")
            with nc.Block() as block:

                @block.vector
                def _(dve):
                    v = nc.vector
                    for signal, per in ((arg_ready, NCH), (norm_ready, 1), (steps, NA - PE_N + 3), (h_done, 1)):
                        dve.sem_inc(signal, 2 * per)
                    dve.wait_ge(a_loaded, 16)
                    dve.wait_ge(rows_loaded, 64)

                    def front(t, par, turn):
                        dve.wait_ge(sum_done, upto(t - 2))
                        v.tensor_scalar(tile_of(xc, t), tile_of(xc, t), in_mean[:, bass.ds(t, 1)],
                                                          in_rstd[:, bass.ds(t, 1)], op0=ALU.subtract, op1=ALU.mult).then_inc(norm_ready, 1)
                        for c in range(NCH):
                            ns = slice(c * PER, (c + 1) * PER)
                            v.tensor_scalar(
                                e[:, par, ns].rearrange("p n i -> p (n i)"), ab[:, c * PER * DI:(c + 1) * PER * DI],
                                delta[:, bass.ds(t, 1)], LOG_FLOOR, op0=ALU.mult, op1=ALU.max).then_inc(arg_ready, 1)

                    def back(t, par, turn):
                        dve.wait_ge(y_turned, upto(t - 2))
                        dve.wait_ge(e_ready, upto(t, NCH))
                        a = acc[:, par]
                        for k, n in enumerate(range(PE_N, NA)):
                            if k:
                                dve.wait_ge(steps, upto(t, NA - PE_N + 3, k))
                            v.scalar_tensor_tensor(
                                a, e[:, par, n], bc[:, bass.ds(t, 1), n:n + 1].rearrange("p a b -> p (a b)"),
                                a if k else d_row[:], op0=ALU.mult, op1=ALU.add).then_inc(steps, 1)
                        k = NA - PE_N
                        dve.wait_ge(steps, upto(t, NA - PE_N + 3, k))
                        dve.wait_ge(sum_done, upto(t))
                        v.tensor_tensor(a, a, s_ps[par][:], ALU.add).then_inc(steps, 1)
                        dve.wait_ge(steps, upto(t, NA - PE_N + 3, k + 1))
                        dve.wait_ge(xh_ready, upto(t, 2))
                        v.tensor_tensor(a, a, tile_of(xc, t), ALU.mult).then_inc(steps, 1)
                        dve.wait_ge(steps, upto(t, NA - PE_N + 3, k + 2))
                        v.tensor_tensor(a, a, tile_of(sz, t), ALU.mult).then_inc(steps, 1)

                    def late(t, par, turn):
                        dve.wait_ge(o_done, upto(t))
                        v.tensor_tensor(tile_of(h, t), tile_of(h, t), o_ps[:, 0:DM], ALU.add).then_inc(h_done, 1)

                    pipelined3(dve, NT, front, back, late)

                @block.scalar
                def _(act):
                    act.sem_inc(e_ready, 2 * NCH)
                    act.sem_inc(yt_ready, 2)

                    def front(t, par, turn):
                        for c in range(NCH):
                            act.wait_ge(arg_ready, upto(t, NCH, c + 1))
                            part = e[:, par, c * PER:(c + 1) * PER]
                            nc.scalar.activation(part, part, ACT.Exp).then_inc(e_ready, 1)

                    def late(t, par, turn):
                        act.wait_ge(y_turned, upto(t))
                        act.wait_ge(o_done, upto(t - 1))
                        nc.scalar.copy(yt[:], y_ps[:]).then_inc(yt_ready, 1)

                    pipelined3(act, NT, front, nothing, late, late_first=True)

                @block.gpsimd
                def _(pool):
                    g = nc.gpsimd
                    pool.sem_inc(diag_ready, 2)
                    pool.sem_inc(xh_ready, 2 * 2)
                    pool.wait_ge(rows_loaded, 64)

                    def front(t, par, turn):
                        pool.wait_ge(sum_done, upto(t - 2))
                        pool.sem_inc(apart, 1)
                        b = bc[:, bass.ds(t, 1), 0:PE_N].rearrange("p a b -> p (a b)")
                        g.tensor_tensor(diag[:, par], spread(ident[:], 1, PE_N), spread(b, 2, P), ALU.mult).then_inc(diag_ready, 1)

                    def back(t, par, turn):
                        pool.wait_ge(norm_ready, upto(t))
                        pool.sem_inc(apart, 1)
                        g.tensor_tensor(tile_of(xc, t), tile_of(xc, t), g_row[:], ALU.mult).then_inc(xh_ready, 1)
                        pool.wait_ge(xh_ready, upto(t, 2, 1))
                        pool.sem_inc(apart, 1)
                        g.tensor_tensor(tile_of(xc, t), tile_of(xc, t), b_row[:], ALU.add).then_inc(xh_ready, 1)

                    pipelined3(pool, NT, front, back, nothing)

                @block.tensor
                def _(pe):
                    mm = nc.tensor.matmul
                    for signal, per in ((sum_done, 1), (y_turned, 1), (o_done, 1)):
                        pe.sem_inc(signal, 2 * per)

                    def front(t, par, turn):
                        pe.wait_ge(diag_ready, upto(t))
                        pe.wait_ge(steps, upto(t - 2, NA - PE_N + 3))
                        for n in range(PE_N):
                            if n % PER == 0:
                                pe.wait_ge(e_ready, upto(t, NCH, n // PER + 1))
                            last = mm(s_ps[par][:], diag[:, par, n], e[:, par, n], start=n == 0, stop=n == PE_N - 1)
                        last.then_inc(sum_done, 1)

                    def back(t, par, turn):
                        pe.wait_ge(steps, upto(t, NA - PE_N + 3))
                        pe.wait_ge(yt_ready, upto(t - 1))
                        for m in range(IC):
                            last = nc.tensor.transpose(y_ps[:, m], acc[:, par, m * P:(m + 1) * P], ident[:])
                        last.then_inc(y_turned, 1)

                    def late(t, par, turn):
                        pe.wait_ge(yt_ready, upto(t))
                        pe.wait_ge(h_done, upto(t - 1))
                        for m in range(IC):
                            last = mm(o_ps[:, 0:DM], yt[:, m], wo[:, m], start=m == 0, stop=m == IC - 1)
                        last.then_inc(o_done, 1)

                    pipelined3(pe, NT, front, back, late, late_first=True)


def pick(nc, dve, made, one, total, out, logits, iota_e, top, cand, first, n):
    v = nc.vector
    v.tensor_reduce(top, logits, AX.X, ALU.max).then_inc(made, one())
    dve.wait_ge(made, total())
    v.tensor_tensor(cand, logits, spread(top, 2, n), ALU.not_equal).then_inc(made, one())
    dve.wait_ge(made, total())
    v.scalar_tensor_tensor(cand, cand, float(n), iota_e, op0=ALU.mult, op1=ALU.add).then_inc(made, one())
    dve.wait_ge(made, total())
    v.tensor_reduce(first, cand, AX.X, ALU.min).then_inc(made, one())
    dve.wait_ge(made, total())
    v.tensor_tensor(out, iota_e, spread(first, 2, n), ALU.is_equal).then_inc(made, one())
    dve.wait_ge(made, total())


def experts(nc, h, ident, strict, ones, stage, router_w, router_b, capacity, groups, w1, b1, w2, b2, gelu,
            sorted_x, sorted_y, out=None):
    NBLK = NTOK // P + groups - 1
    G = groups
    with ExitStack() as ctx:
        sb, ps, sem = memory(nc, ctx, stage)
        dest = sb("dest", [P, NT], I32)
        prob = sb("prob", [P, NT])
        owner = sb("owner", [P, NBLK], I32)
        xn = sb("xn", [P, NT, DM])
        zeroed = sem("zeroed")
        scattered = sem("scattered")
        with ExitStack() as ctx2:
            sb, ps, sem = memory(nc, ctx2, stage + "a")
            xb = sb("xb", [P, 2, DM])
            xt = sb("xt", [P, 2, DC, P])
            rw = sb("rw", [P, DC, NE])
            rb = sb("rb", [P, NE])
            logits = sb("logits", [P, NT, NE])
            zeros = sb("zeros", [P, DM])
            iota_e = sb("iota_e", [P, NT, NE])
            full = sb("full", [P, G, NTOK // P])
            strict_h = sb("strict_h", [P, P], BF16)
            ones_h = sb("ones_h", [P, P], BF16)
            block_no = sb("block_no", [P, NBLK, G - 1])
            t_ps = [ps(f"t_ps{i}", [P, 512]) for i in range(2)]
            l_ps = [ps(f"l_ps{i}", [P, 512]) for i in range(2)]
            mean, rstd = row_stats(nc, ctx2, stage + "_ln", h)
            loaded, zero_made, tables = sem("loaded"), sem("zero_made"), sem("tables")
            xb_ready, x_turned, xt_ready, l_done, l_moved, copied = (
                sem(n) for n in ("xb_ready", "x_turned", "xt_ready", "l_done", "l_moved", "copied"))
            with nc.Block() as block:

                @block.sync
                def _(sp):
                    sp.dma_start(rw[:], router_w.rearrange("(c p) e -> p c e", p=P)).then_inc(loaded, 16)
                    sp.dma_start(rb[:], router_b.partition_broadcast(P)).then_inc(loaded, 16)
                    sp.wait_ge(zero_made, 1)
                    sp.dma_start(sorted_x.rearrange("(b p) d -> p b d", p=P), spread(zeros[:], 1, NBLK)).then_inc(zeroed, 16)

                @block.gpsimd
                def _(pool):
                    g = nc.gpsimd
                    pool.sem_inc(copied, 2)
                    for e in range(NE):
                        g.memset(iota_e[:, :, e:e + 1], float(e)).then_inc(tables, 1)
                    for k in range(NTOK // P):
                        g.memset(full[:, :, k:k + 1], float(k * P)).then_inc(tables, 1)
                    for j in range(NBLK):
                        g.memset(block_no[:, j], float(j)).then_inc(tables, 1)
                    g.tensor_copy(strict_h[:], strict[:]).then_inc(tables, 1)
                    g.tensor_copy(ones_h[:], ones[:]).then_inc(tables, 1)
                    with pool.Fori(0, NT // 2) as i:
                        for par in range(2):
                            pool.wait_ge(xb_ready, upto(2 * i + par))
                            pool.wait_ge(tables, 1)
                            g.tensor_copy(tile_of(xn, 2 * i + par), xb[:, par]).then_inc(copied, 1)

                @block.vector
                def _(dve):
                    v = nc.vector
                    dve.sem_inc(xb_ready, 2)
                    dve.sem_inc(l_moved, 2)
                    v.memset(zeros[:], 0.0).then_inc(zero_made, 1)
                    dve.wait_ge(loaded, 32)

                    def front(t, par, turn):
                        dve.wait_ge(copied, upto(t - 2))
                        dve.wait_ge(x_turned, upto(t - 2))
                        v.tensor_scalar(xb[:, par], tile_of(h, t), mean[:, bass.ds(t, 1)],
                                                        rstd[:, bass.ds(t, 1)], op0=ALU.subtract, op1=ALU.mult).then_inc(xb_ready, 1)

                    def late(t, par, turn):
                        dve.wait_ge(l_done, upto(t))
                        v.tensor_tensor(tile_of(logits, t), l_ps[par][:, 0:NE], rb[:], ALU.add).then_inc(l_moved, 1)

                    pipelined3(dve, NT, front, nothing, late)

                @block.scalar
                def _(act):
                    act.sem_inc(xt_ready, 2)
                    with act.Fori(0, NT // 2) as i:
                        for par in range(2):
                            t = 2 * i + par
                            act.wait_ge(l_done, upto(t - 2))
                            act.wait_ge(x_turned, upto(t))
                            nc.scalar.copy(xt[:, par].rearrange("p c n -> p (c n)"), t_ps[par][:, 0:DM]).then_inc(xt_ready, 1)

                @block.tensor
                def _(pe):
                    pe.sem_inc(x_turned, 2)
                    pe.sem_inc(l_done, 2)
                    pe.wait_ge(loaded, 32)

                    def front(t, par, turn):
                        pe.wait_ge(xt_ready, upto(t - 2))
                        pe.wait_ge(xb_ready, upto(t))
                        for c in range(DC):
                            last = nc.tensor.transpose(t_ps[par][:, c * P:(c + 1) * P], xb[:, par, c * P:(c + 1) * P], ident[:])
                        last.then_inc(x_turned, 1)

                    def back(t, par, turn):
                        pe.wait_ge(l_moved, upto(t - 2))
                        pe.wait_ge(xt_ready, upto(t))
                        for c in range(DC):
                            last = nc.tensor.matmul(l_ps[par][:, 0:NE], xt[:, par, c], rw[:, c], start=c == 0, stop=c == DC - 1)
                        last.then_inc(l_done, 1)

                    pipelined3(pe, NT, front, back, nothing)

            sb, ps, sem = memory(nc, ctx2, stage + "b")
            hot1 = sb("hot1", [P, NT, NE])
            hot2 = sb("hot2", [P, NT, NE])
            hot_h = sb("hot_h", [P, NT, G], BF16)
            work = sb("work", [P, NT, G])
            assign = sb("assign", [P, NT, G])
            top, first, pos, over = (sb(n, [P, NT]) for n in ("top", "first", "pos", "over"))
            per_group = sb("per_group", [P, G])
            used = sb("used", [P, G])
            count = sb("count", [P, G])
            begin = sb("begin", [P, G + 1])
            fit = sb("fit", [P, G, NTOK // P])
            own = sb("own", [P, NBLK, G - 1])
            own_f = sb("own_f", [P, NBLK])
            r_ps = ps("r_ps", [P, 512])
            c_ps = ps("c_ps", [P, 512])
            chain, hot_ready, ranked, exped = (sem(n) for n in ("chain", "hot_ready", "ranked", "exped"))
            rank = r_ps[:, 0:NT * G].rearrange("p (t g) -> p t g", g=G)
            rank_e = rank if G == NE else r_ps[:, 0:NT * NE].rearrange("p (t g) -> p t g", g=NE)
            rounds = [G] if capacity is None else [NE, NE, G]
            with nc.Block() as block:

                @block.tensor
                def _(pe):
                    for k, g in enumerate(rounds):
                        pe.wait_ge(hot_ready, 2 * k + 2)
                        r = r_ps[:, 0:NT * g].rearrange("p (t g) -> p t g", g=g)
                        nc.tensor.matmul(r, strict_h[:], hot_h[:, :, 0:g], start=True, stop=False)
                        for t in range(NT - 1):
                            nc.tensor.matmul(r[:, t + 1:], ones_h[:], spread(hot_h[:, t, 0:g], 1, NT - 1 - t), start=False,
                                             stop=t == NT - 2)
                        nc.tensor.matmul(c_ps[:, 0:g], ones[:], per_group[:, 0:g], start=True, stop=True).then_inc(ranked, 1)

                @block.scalar
                def _(act):
                    if capacity is None:
                        act.wait_ge(exped, 1)
                        nc.scalar.activation(work[:], work[:], ACT.Exp).then_inc(exped, 1)

                @block.vector
                def _(dve):
                    v = nc.vector
                    one, total = counting()
                    turn = [0]

                    def ranks(hot, g):
                        turn[0] += 1
                        v.tensor_copy(hot_h[:, :, 0:g], hot).then_inc(hot_ready, 1)
                        v.tensor_reduce(per_group[:, 0:g], hot[:, :, 0:g].rearrange("p t g -> p g t"), AX.X,
                                        ALU.add).then_inc(hot_ready, 1)
                        dve.wait_ge(ranked, turn[0])

                    def own_rank(out, hot, add):
                        g = hot.shape[2]
                        w = work[:, :, 0:g]
                        r = r_ps[:, 0:NT * g].rearrange("p (t g) -> p t g", g=g)
                        if add is None:
                            v.tensor_tensor(w, r, hot, ALU.mult).then_inc(chain, one())
                            dve.wait_ge(chain, total())
                        else:
                            v.tensor_tensor(w, r, spread(add, 1, NT), ALU.add).then_inc(chain, one())
                            dve.wait_ge(chain, total())
                            v.tensor_tensor(w, w, hot, ALU.mult).then_inc(chain, one())
                            dve.wait_ge(chain, total())
                        v.tensor_reduce(out, w, AX.X, ALU.add).then_inc(chain, one())
                        dve.wait_ge(chain, total())

                    if capacity is None:
                        pick(nc, dve, chain, one, total, assign[:], logits[:], iota_e[:], top[:], work[:], first[:], NE)
                        v.tensor_tensor(work[:], logits[:], spread(top[:], 2, NE), ALU.subtract).then_inc(exped, 1)
                        dve.wait_ge(exped, 2)
                        v.tensor_reduce(prob[:], work[:], AX.X, ALU.add).then_inc(chain, one())
                        dve.wait_ge(chain, total())
                        v.reciprocal(prob[:], prob[:]).then_inc(chain, one())
                        dve.wait_ge(chain, total())
                        ranks(assign[:], NE)
                    else:
                        w8 = work[:, :, 0:NE]
                        pick(nc, dve, chain, one, total, hot1[:], logits[:], iota_e[:], top[:], w8, first[:], NE)
                        v.scalar_tensor_tensor(logits[:], hot1[:], -3e38, logits[:], op0=ALU.mult, op1=ALU.add).then_inc(chain, one())
                        dve.wait_ge(chain, total())
                        pick(nc, dve, chain, one, total, hot2[:], logits[:], iota_e[:], top[:], w8, first[:], NE)
                        ranks(hot1[:], NE)
                        v.tensor_scalar(used[:, 0:NE], c_ps[:, 0:NE], float(capacity), None, op0=ALU.min).then_inc(chain, one())
                        own_rank(pos[:], hot1[:], None)
                        v.tensor_scalar(over[:], pos[:], float(capacity), None, op0=ALU.is_ge).then_inc(chain, one())
                        dve.wait_ge(chain, total())
                        v.tensor_tensor(assign[:, :, 0:NE], hot2[:], spread(over[:], 2, NE), ALU.mult).then_inc(chain, one())
                        dve.wait_ge(chain, total())
                        ranks(assign[:, :, 0:NE], NE)
                        own_rank(pos[:], hot2[:], used[:, 0:NE])
                        v.tensor_scalar(pos[:], pos[:], float(capacity), None, op0=ALU.is_lt).then_inc(chain, one())
                        dve.wait_ge(chain, total())
                        v.tensor_tensor(pos[:], pos[:], over[:], ALU.mult).then_inc(chain, one())
                        dve.wait_ge(chain, total())
                        v.tensor_tensor(hot2[:], hot2[:], spread(pos[:], 2, NE), ALU.mult).then_inc(chain, one())
                        v.tensor_tensor(assign[:, :, NE], over[:], pos[:], ALU.subtract).then_inc(chain, one())
                        v.tensor_scalar(over[:], over[:], -1.0, 1.0, op0=ALU.mult, op1=ALU.add).then_inc(chain, one())
                        dve.wait_ge(chain, total())
                        v.tensor_tensor(hot1[:], hot1[:], spread(over[:], 2, NE), ALU.mult).then_inc(chain, one())
                        dve.wait_ge(chain, total())
                        v.tensor_tensor(assign[:, :, 0:NE], hot1[:], hot2[:], ALU.add).then_inc(chain, one())
                        dve.wait_ge(chain, total())
                        ranks(assign[:], G)
                    v.tensor_tensor(fit[:], spread(c_ps[:, 0:G], 2, NTOK // P), full[:], ALU.is_gt).then_inc(chain, one())
                    dve.wait_ge(chain, total())
                    v.memset(begin[:, 0:1], 0.0).then_inc(chain, one())
                    v.tensor_reduce(count[:], fit[:], AX.X, ALU.add).then_inc(chain, one())
                    dve.wait_ge(chain, total())
                    for g in range(G):
                        v.tensor_tensor(begin[:, g + 1:g + 2], begin[:, g:g + 1], count[:, g:g + 1], ALU.add).then_inc(chain, one())
                        dve.wait_ge(chain, total())
                    v.tensor_tensor(own[:], block_no[:], spread(begin[:, 1:G], 1, NBLK), ALU.is_ge).then_inc(chain, one())
                    v.tensor_scalar(used[:], begin[:, 0:G], float(P), None, op0=ALU.mult).then_inc(chain, one())
                    dve.wait_ge(chain, total())
                    v.tensor_reduce(own_f[:], own[:], AX.X, ALU.add).then_inc(chain, one())
                    dve.wait_ge(chain, total())
                    v.tensor_copy(owner[:], own_f[:])
                    own_rank(pos[:], assign[:], used[:])
                    v.tensor_copy(dest[:], pos[:])

        with ExitStack() as ctx3:
            sb, ps, sem = memory(nc, ctx3, stage + "c")
            wa = sb("wa", [P, 2, DC, FF])
            wb = sb("wb", [P, 2, FC, DM])
            ba = sb("ba", [P, 2, FC])
            bb = sb("bb", [P, 2, DM])
            x = sb("x", [P, 2, DM])
            xt = sb("xt", [P, 2, DC, P])
            hid = sb("hid", [P, 2, FC, P])
            y = sb("y", [P, 2, DM])
            t_ps = [ps(f"t_ps{i}", [P, 512]) for i in range(2)]
            h_ps = [ps(f"h_ps{i}", [P, FC, P]) for i in range(2)]
            y_ps = [ps(f"y_ps{i}", [P, 512]) for i in range(2)]
            wa_loaded = [sem(f"wa_loaded{i}") for i in range(2)]
            wb_loaded = [sem(f"wb_loaded{i}") for i in range(2)]
            x_loaded = [sem(f"x_loaded{i}") for i in range(2)]
            y_stored = [sem(f"y_stored{i}") for i in range(2)]
            x_turned, xt_ready, y_done, y_ready = (sem(n) for n in ("x_turned", "xt_ready", "y_done", "y_ready"))
            h_done, hid_ready = sem("h_done"), sem("hid_ready")
            xs, ys = (a.rearrange("(b p) d -> b p d", p=P) for a in (sorted_x, sorted_y))
            with nc.Block() as block:

                @block.gpsimd
                def _(pool):
                    pool.wait_ge(zeroed, 16)
                    for t in range(NT):
                        nc.gpsimd.indirect_dma_start(
                            sorted_x, bass.IndirectOffsetOnAxis(ap=dest[:, t:t + 1].bitcast(U32), axis=0), xn[:, t, :],
                            None).then_inc(scattered, 16)
                    pool.wait_ge(scattered, 16 * NT)

                @block.sync
                def _(sp):
                    for par in range(2):
                        sp.sem_inc(wa_loaded[par], 2 * 32)
                        sp.sem_inc(wb_loaded[par], 2 * 32)
                        sp.sem_inc(x_loaded[par], 2 * 16)

                    def rows(j, par, turn):
                        sp.wait_ge(x_turned, upto(j - 2))
                        sp.dma_start(x[:, par], xs[bass.ds(j, 1)].rearrange("a p d -> p (a d)")).then_inc(x_loaded[par], 16)

                    def weights(j, par, turn):
                        e = sp.value_load(owner[0:1, bass.ds(j, 1)], min_val=0, max_val=G - 1)
                        sp.wait_ge(h_done, upto(j - 2, 2))
                        sp.wait_ge(hid_ready, upto(j - 2, FC))
                        pick_e = lambda a: a[bass.ds(e, 1)]
                        sp.dma_start(
                            wa[:, par], pick_e(w1).rearrange("e (c p) n -> p (e c) n", p=P)).then_inc(wa_loaded[par], 16)
                        sp.dma_start(ba[:, par], pick_e(b1).rearrange("e p c -> p (e c)")).then_inc(wa_loaded[par], 16)
                        sp.wait_ge(y_done, upto(j - 2))
                        sp.wait_ge(y_ready, upto(j - 2))
                        sp.dma_start(
                            wb[:, par], pick_e(w2).rearrange("e (c p) n -> p (e c) n", p=P)).then_inc(wb_loaded[par], 16)
                        sp.dma_start(
                            bb[:, par], pick_e(b2).rearrange("e d -> (e d)").partition_broadcast(P)).then_inc(wb_loaded[par], 16)

                    weights(0, 0, 0)
                    sp.wait_ge(scattered, 16 * NT)
                    rows(0, 0, 0)
                    rows(1, 1, 0)
                    with sp.Fori(0, (NBLK - 2) // 2) as i:
                        rows(2 * i + 2, 0, i + 1)
                        weights(2 * i + 1, 1, i)
                        rows(2 * i + 3, 1, i + 1)
                        weights(2 * i + 2, 0, i + 1)
                    if NBLK % 2:
                        rows(NBLK - 1, 0, NBLK // 2)
                        weights(NBLK - 2, 1, NBLK // 2 - 1)
                    weights(NBLK - 1, (NBLK - 1) % 2, (NBLK - 1) // 2)

                @block.vector
                def _(dve):
                    v = nc.vector
                    dve.sem_inc(xt_ready, 2)
                    dve.sem_inc(y_ready, 2)

                    def front(j, par, turn):
                        dve.wait_ge(h_done, upto(j - 2, 2))
                        dve.wait_ge(x_turned, upto(j))
                        v.tensor_copy(xt[:, par].rearrange("p c n -> p (c n)"), t_ps[par][:, 0:DM]).then_inc(xt_ready, 1)

                    def late(j, par, turn):
                        dve.wait_ge(wb_loaded[par], upto(turn, 32))
                        dve.wait_ge(y_stored[par], upto(turn - 1, 16))
                        dve.wait_ge(y_done, upto(j))
                        v.tensor_tensor(y[:, par], y_ps[par][:, 0:DM], bb[:, par], ALU.add).then_inc(y_ready, 1)

                    pipelined3(dve, NBLK, front, nothing, late)

                @block.scalar
                def _(act):
                    act.sem_inc(hid_ready, 2 * FC)
                    for par in range(2):
                        act.sem_inc(y_stored[par], 2 * 16)

                    def front(j, par, turn):
                        act.wait_ge(wa_loaded[par], upto(turn, 32))
                        act.wait_ge(y_done, upto(j - 2))
                        for m in range(FC):
                            if m % (FC // 2) == 0:
                                act.wait_ge(h_done, upto(j, 2, 1 + m // (FC // 2)))
                            nc.scalar.activation(hid[:, par, m], h_ps[par][:, m], gelu,
                                                                  bias=ba[:, par, m:m + 1]).then_inc(hid_ready, 1)

                    def back(j, par, turn):
                        act.wait_ge(y_ready, upto(j))
                        act.dma_start(ys[bass.ds(j, 1)].rearrange("a p d -> p (a d)"), y[:, par]).then_inc(y_stored[par], 16)

                    pipelined(act, NBLK, front, back)
                    for par in range(2):
                        act.wait_ge(y_stored[par], upto((NBLK - 1 - par) // 2, 16))

                @block.tensor
                def _(pe):
                    mm = nc.tensor.matmul
                    for signal, per in ((x_turned, 1), (h_done, 2), (y_done, 1)):
                        pe.sem_inc(signal, 2 * per)

                    def front(j, par, turn):
                        pe.wait_ge(xt_ready, upto(j - 2))
                        pe.wait_ge(x_loaded[par], upto(turn, 16))
                        for c in range(DC):
                            last = nc.tensor.transpose(t_ps[par][:, c * P:(c + 1) * P], x[:, par, c * P:(c + 1) * P], ident[:])
                        last.then_inc(x_turned, 1)

                    def back(j, par, turn):
                        pe.wait_ge(wa_loaded[par], upto(turn, 32))
                        pe.wait_ge(hid_ready, upto(j - 2, FC))
                        pe.wait_ge(xt_ready, upto(j))
                        for m in range(FC):
                            for c in range(DC):
                                last = mm(h_ps[par][:, m], wa[:, par, c, m * P:(m + 1) * P], xt[:, par, c],
                                          start=c == 0, stop=c == DC - 1)
                            if m % (FC // 2) == FC // 2 - 1:
                                last.then_inc(h_done, 1)

                    def late(j, par, turn):
                        pe.wait_ge(wb_loaded[par], upto(turn, 32))
                        pe.wait_ge(y_ready, upto(j - 2))
                        pe.wait_ge(hid_ready, upto(j, FC))
                        for m in range(FC):
                            last = mm(y_ps[par][:, 0:DM], hid[:, par, m], wb[:, par, m], start=m == 0, stop=m == FC - 1)
                        last.then_inc(y_done, 1)

                    pipelined3(pe, NBLK, front, back, late)

        with ExitStack() as ctx4:
            sb, ps, sem = memory(nc, ctx4, stage + "d")
            yg = sb("yg", [P, NT, DM])
            gathered = [sem(f"gathered{i}") for i in range(2)]
            added, sent = sem("added"), sem("sent")
            with nc.Block() as block:

                @block.gpsimd
                def _(pool):
                    for t in range(NT):
                        nc.gpsimd.indirect_dma_start(
                            yg[:, t, :], None, sorted_y,
                            bass.IndirectOffsetOnAxis(ap=dest[:, t:t + 1].bitcast(U32), axis=0)).then_inc(gathered[t // 8], 16)

                @block.vector
                def _(dve):
                    for t in range(NT):
                        if t % 8 == 0:
                            dve.wait_ge(gathered[t // 8], 128)
                        scale = prob[:, t:t + 1] if capacity is None else 1.0
                        nc.vector.scalar_tensor_tensor(h[:, t], yg[:, t], scale, h[:, t], op0=ALU.mult,
                                                       op1=ALU.add).then_inc(added, 1)

                if out is not None:
                    @block.sync
                    def _(sp):
                        for k in range(4):
                            sp.wait_ge(added, 4 * k + 4)
                            sp.dma_start(out.rearrange("(t p) d -> p t d", p=P)[:, 4 * k:4 * k + 4],
                                         h[:, 4 * k:4 * k + 4]).then_inc(sent, 16)
                        sp.wait_ge(sent, 64)


def attention(nc, h, ident, ident_h, w_qkv, w_o, rope):
    UNITS = NH // 2
    HG = NH // 4
    SW = P + SEQ
    VW = DK + 1
    with ExitStack() as ctx:
        sb, ps, sem = memory(nc, ctx, "attn")
        mean, rstd = row_stats(nc, ctx, "ln2", h)
        wqkv = sb("wqkv", [P, DC, 3 * DM])
        wo = sb("wo", [P, DC, DM])
        table = sb("table", [P, 2, TPB, DK])
        mask = sb("mask", [P, P])
        mask_h = sb("mask_h", [P, P], BF16)
        xn = sb("xn", [P, TPB, DM])
        xt = sb("xt", [P, DC, SEQ])
        t1 = sb("t1", [P, TPB, 2 * NH, DK])
        t2 = sb("t2", [P, TPB, 2 * NH, DK])
        qk = sb("qk", [P, TPB, 2, HG, 4, 32])
        qkt = sb("qkt", [P, 2, HG, 2, SEQ])
        head_mask = sb("head_mask", [P, 4])
        qm = sb("qm", [P, 2, HG, 4, SEQ])
        v = sb("v", [P, 2, TPB, NH, VW])
        neg = sb("neg", [P, 2, TPB, 2])
        prob = sb("prob", [P, 2, 2, SW])
        probt = sb("probt", [P, 2, 2, SW])
        rec = sb("rec", [P, 2, 2, TPB])
        at = sb("at", [P, TPB, DM])
        ot = sb("ot", [P, DC, SEQ])
        s_ps = [ps(f"s_ps{i}", [P, 2, 512]) for i in range(2)]
        p_ps = [ps(f"p_ps{i}", [P, 512]) for i in range(2)]
        f_ps = ps("f_ps", [P, 512])
        o_ps = ps("o_ps", [P, 512])
        loaded, made = sem("loaded"), sem("made")
        xn_ready = sem("xn_ready")
        piece_done = sem("piece_done")
        by_act = sem("by_act")
        by_dve = sem("by_dve")
        roped = sem("roped")
        masked = sem("masked")
        scored = sem("scored")
        max_ready = sem("max_ready")
        exp_ready = sem("exp_ready")
        p_turned = sem("p_turned")
        pt_dve, pt_act = sem("pt_dve"), sem("pt_act")
        weighed = sem("weighed")
        at_ready = sem("at_ready")
        o_turned, ot_ready, o_done, h_done = (sem(n) for n in ("o_turned", "ot_ready", "o_done", "h_done"))

        def batches(eng, pieces, step, finish):
            pieces(0, 0)
            step(0, 0, True, False)
            with eng.Fori(0, NB // 2 - 1) as i:
                step(2 * i + 1, 1, False, False)
                step(2 * i + 2, 0, False, False)
            step(NB - 1, 1, False, True)
            finish(NB - 1)

        with nc.Block() as block:

            @block.sync
            def _(sp):
                sp.dma_start(wqkv[:], w_qkv.rearrange("(c p) n -> p c n", p=P)).then_inc(loaded, 16)
                sp.dma_start(wo[:], w_o.rearrange("(c p) n -> p c n", p=P)).then_inc(loaded, 16)
                sp.dma_start(table[:], rope.rearrange("f (k p) d -> p f k d", p=P)).then_inc(loaded, 16)

            @block.gpsimd
            def _(pool):
                g = nc.gpsimd
                pool.sem_inc(roped, 2 * TPB)
                pool.sem_inc(masked, 2 * HG)
                one, total = counting()
                g.memset(v[:], 1.0).then_inc(made, one())
                g.memset(qk[:], 0.0).then_inc(made, one())
                g.memset(mask[:], 0.0).then_inc(made, one())
                pool.wait_ge(made, total())
                g.affine_select(out=mask[:], in_=mask[:], compare_op=ALU.is_ge, fill=-1e30, base=0,
                                      pattern=[[-1, P]], channel_multiplier=1).then_inc(made, one())
                pool.wait_ge(made, total())
                g.tensor_copy(mask_h[:], mask[:]).then_inc(made, one())
                g.memset(head_mask[:], 0.0).then_inc(made, one())
                pool.wait_ge(made, total())
                for j in range(4):
                    g.memset(head_mask[32 * j:32 * j + 32, j:j + 1], 1.0).then_inc(made, one())
                pool.wait_ge(made, total())

                def mask_heads(b, par, again):
                    if again:
                        pool.wait_ge(scored, upto(8 * (b - 2) + 7))
                    for a in range(HG):
                        if a % 2:
                            pool.wait_ge(by_dve, upto(b, 8, 7 + a // 2))
                        else:
                            pool.wait_ge(by_act, upto(b, 4, 3 + a // 2))
                        g.tensor_tensor(qm[:, par, a], spread(qkt[:, par, a, 0], 1, 4),
                                        spread(head_mask[:], 2, SEQ), ALU.mult).then_inc(masked, 1)

                def rope_sum(b):
                    for k in range(TPB):
                        pool.wait_ge(by_dve, upto(b, 8, 3 * k + 3))
                        pool.wait_ge(piece_done, upto(b - 1, 8, 8))
                        g.tensor_tensor(qk[:, k].rearrange("p f a c d -> p (f a c) d")[:, :, 0:DK],
                                                     t1[:, k], t2[:, k], ALU.add).then_inc(roped, 1)

                def step(b, par, first, last):
                    if not last:
                        rope_sum(b + 1)
                        mask_heads(b + 1, 1 - par, not first)

                def pieces(b, par):
                    rope_sum(b)
                    mask_heads(b, par, False)

                batches(pool, pieces, step, lambda b: None)

            @block.vector
            def _(dve):
                vv = nc.vector
                for signal, per in ((xn_ready, TPB), (by_dve, 8), (max_ready, 3), (pt_dve, 1), (at_ready, 4), (h_done, 1)):
                    dve.sem_inc(signal, 2 * per)
                dve.wait_ge(made, 10)
                dve.wait_ge(loaded, 48)

                def rows(b):
                    dve.wait_ge(piece_done, upto(b - 1, 8, 1))
                    for k in range(TPB):
                        t = TPB * b + k
                        vv.tensor_scalar(xn[:, k], tile_of(h, t), mean[:, bass.ds(t, 1)],
                                                         rstd[:, bass.ds(t, 1)], op0=ALU.subtract, op1=ALU.mult).then_inc(xn_ready, 1)

                def piece(b, par, u):
                    if u in (1, 2):
                        k = u - 1
                        dve.wait_ge(roped, upto(b - 1, TPB, k + 1))
                        dve.wait_ge(piece_done, upto(b, 8, u + 1))
                        x = f_ps[:, 0:512].rearrange("p (g d) -> p g d", d=DK)
                        vv.tensor_tensor(t1[:, k], x, spread(table[:, 0, k], 1, 2 * NH), ALU.mult).then_inc(by_dve, 1)
                        for o in range(2):
                            vv.tensor_tensor(t2[:, k, :, o::2], x[:, :, 1 - o::2],
                                                           spread(table[:, 1, k, o::2], 1, 2 * NH), ALU.mult).then_inc(by_dve, 1)
                    elif u in (5, 7):
                        dve.wait_ge(piece_done, upto(b, 8, u + 1))
                        vv.tensor_copy(qkt[:, par, u - 4].rearrange("p f s -> p (f s)"), f_ps[:]).then_inc(by_dve, 1)

                def maximum(w, ub):
                    dve.wait_ge(scored, upto(w))
                    dve.wait_ge(exp_ready, upto(w - 2, 4))
                    vv.tensor_reduce(neg[:, ub, 0], s_ps[ub][:, :, 0:P], AX.X, ALU.max).then_inc(max_ready, 1)
                    vv.tensor_reduce(neg[:, ub, 1], s_ps[ub][:, :, P:SW], AX.X, ALU.max).then_inc(max_ready, 1)
                    dve.wait_ge(max_ready, upto(w, 3, 2))
                    vv.tensor_scalar(neg[:, ub], neg[:, ub], -DK ** -0.5, None, op0=ALU.mult).then_inc(max_ready, 1)

                def turned(b, u):
                    w, ub = 8 * b + u, u % 2
                    dve.wait_ge(p_turned, upto(w, 2, 1))
                    dve.wait_ge(weighed, upto(w - 2))
                    vv.tensor_copy(probt[:, ub, 0], p_ps[0][:, 0:SW]).then_inc(pt_dve, 1)

                def divide(b, u):
                    w, ub = 8 * b + u, u % 2
                    dve.wait_ge(weighed, upto(w))
                    s = [p_ps[j][:, SW:SW + TPB * VW].rearrange("p (k d) -> p k d", d=VW) for j in range(2)]
                    for j in range(2):
                        vv.reciprocal(rec[:, ub, j], s[j][:, :, DK]).then_inc(at_ready, 1)
                    dve.wait_ge(o_turned, upto(b - 1))
                    for j in range(2):
                        dve.wait_ge(at_ready, upto(w, 4, 1 + j))
                        vv.tensor_tensor(at[:, :, (2 * u + j) * DK:(2 * u + j + 1) * DK], s[j][:, :, 0:DK],
                                         spread(rec[:, ub, j], 2, DK), ALU.mult).then_inc(at_ready, 1)

                def add(b):
                    dve.wait_ge(o_done, upto(b))
                    hb = h[:, bass.ds(TPB * b, TPB)].rearrange("p k d -> p (k d)")
                    vv.tensor_tensor(hb, hb, o_ps[:], ALU.add).then_inc(h_done, 1)

                def pieces(b, par):
                    rows(b)
                    for u in range(8):
                        piece(b, par, u)
                    maximum(0, 0)
                    maximum(1, 1)

                def step(b, par, first, last):
                    if not last:
                        rows(b + 1)
                    for u in range(UNITS):
                        turned(b, u)
                        if not (last and u >= UNITS - 2):
                            maximum(8 * b + u + 2, u % 2)
                        divide(b, u)
                        if u == 2 and not first:
                            add(b - 1)
                        if not last:
                            piece(b + 1, 1 - par, u)

                batches(dve, pieces, step, add)

            @block.scalar
            def _(act):
                for signal, per in ((by_act, 4), (exp_ready, 4), (pt_act, 1), (ot_ready, 1)):
                    act.sem_inc(signal, 2 * per)
                act.wait_ge(made, 10)

                def piece(b, par, u):
                    if u not in (0, 3, 4, 6):
                        return
                    act.wait_ge(piece_done, upto(b, 8, u + 1))
                    if u == 0:
                        act.wait_ge(piece_done, upto(b - 1, 8, 4))
                        nc.scalar.copy(xt[:].rearrange("p c s -> p (c s)"), f_ps[:]).then_inc(by_act, 1)
                    elif u == 3:
                        nc.scalar.copy(v[:, par, :, :, 0:DK],
                                                     f_ps[:].rearrange("p (k a d) -> p k a d", k=TPB, d=DK)).then_inc(by_act, 1)
                    else:
                        nc.scalar.copy(qkt[:, par, u - 4].rearrange("p f s -> p (f s)"), f_ps[:]).then_inc(by_act, 1)

                def exps(w, ub):
                    act.wait_ge(max_ready, upto(w, 3))
                    act.wait_ge(p_turned, upto(w - 2, 2))
                    for j in range(2):
                        for k, cols in enumerate((slice(0, P), slice(P, SW))):
                            nc.scalar.activation(prob[:, ub, j, cols], s_ps[ub][:, j, cols], ACT.Exp,
                                                                  bias=neg[:, ub, k, j:j + 1], scale=DK ** -0.5).then_inc(exp_ready, 1)

                def unit(b, u):
                    w, ub = 8 * b + u, u % 2
                    act.wait_ge(p_turned, upto(w, 2, 2))
                    act.wait_ge(weighed, upto(w - 2))
                    nc.scalar.copy(probt[:, ub, 1], p_ps[1][:, 0:SW]).then_inc(pt_act, 1)

                def output(b):
                    act.wait_ge(o_turned, upto(b))
                    act.wait_ge(o_done, upto(b - 1))
                    nc.scalar.copy(ot[:].rearrange("p c s -> p (c s)"), o_ps[:]).then_inc(ot_ready, 1)

                def pieces(b, par):
                    for u in range(8):
                        piece(b, par, u)
                    exps(0, 0)

                def step(b, par, first, last):
                    for u in range(UNITS):
                        unit(b, u)
                        if not (last and u == UNITS - 1):
                            exps(8 * b + u + 1, (u + 1) % 2)
                        if u == 0 and not first:
                            output(b - 1)
                        if not last:
                            piece(b + 1, 1 - par, u)

                batches(act, pieces, step, output)

            @block.tensor
            def _(pe):
                mm = nc.tensor.matmul
                for signal, per in ((piece_done, 8), (scored, 1), (p_turned, 2), (weighed, 1), (o_turned, 1), (o_done, 1)):
                    pe.sem_inc(signal, 2 * per)
                pe.wait_ge(loaded, 48)
                pe.wait_ge(made, 10)

                def piece(b, par, u):
                    if u == 0:
                        pe.wait_ge(by_dve, upto(b - 1, 8))
                    elif u in (2, 3, 6):
                        pe.wait_ge(by_dve, upto(b, 8, {2: 3, 3: 6, 6: 7}[u]))
                    else:
                        pe.wait_ge(by_act, upto(b, 4, {1: 1, 4: 2, 5: 3, 7: 4}[u]))
                    if u == 0:
                        pe.wait_ge(xn_ready, upto(b, TPB))
                        for k in range(TPB):
                            for c in range(DC):
                                last = nc.tensor.transpose(f_ps[:, c * SEQ + k * P:c * SEQ + (k + 1) * P],
                                                           xn[:, k, c * P:(c + 1) * P], ident[:])
                    elif u in (1, 2):
                        k = u - 1
                        for c in range(DC):
                            last = mm(f_ps[:], xt[:, c, k * P:(k + 1) * P], wqkv[:, c, 0:2 * DM], start=c == 0,
                                      stop=c == DC - 1)
                    elif u == 3:
                        for k in range(TPB):
                            for c in range(DC):
                                last = mm(f_ps[:, k * DM:(k + 1) * DM], xt[:, c, k * P:(k + 1) * P],
                                          wqkv[:, c, 2 * DM:], start=c == 0, stop=c == DC - 1)
                    else:
                        pe.wait_ge(roped, upto(b, TPB))
                        for f in range(2):
                            for k in range(TPB):
                                last = nc.tensor.transpose(f_ps[:, f * SEQ + k * P:f * SEQ + (k + 1) * P],
                                                           qk[:, k, f, u - 4].rearrange("p c d -> p (c d)"), ident[:])
                    last.then_inc(piece_done, 1)

                def scores(b, par, u):
                    w, ub, a = 8 * b + u, u % 2, u // 2
                    pe.wait_ge(exp_ready, upto(w - 2, 4))
                    pe.wait_ge(masked, upto(b, HG, a + 1))
                    for j in range(2):
                        q = qm[:, par, a, 2 * (u % 2) + j]
                        k = qkt[:, par, a, 1]
                        s = s_ps[ub][:, j]
                        mm(s[:, 0:P], q[:, 0:P], k[:, 0:P], start=True, stop=False)
                        mm(s[:, 0:P], ident_h[:], mask_h[:], start=False, stop=True)
                        mm(s[:, P:SW], q[:, P:SEQ], k, start=True, stop=False)
                        last = mm(s[:, 2 * P:SW], ident_h[:], mask_h[:], start=False, stop=True)
                    last.then_inc(scored, 1)

                def turn(b, u):
                    w, ub = 8 * b + u, u % 2
                    for j in range(2):
                        pe.wait_ge(at_ready, upto(w - 1, 4, 3 + j))
                        pe.wait_ge(exp_ready, upto(w, 4, 2 * j + 2))
                        for i in range(SW // P):
                            last = nc.tensor.transpose(p_ps[j][:, i * P:(i + 1) * P], prob[:, ub, j, i * P:(i + 1) * P], ident[:])
                        last.then_inc(p_turned, 1)

                def weigh(b, par, u):
                    w, ub = 8 * b + u, u % 2
                    pe.wait_ge(by_act, upto(b, 4, 2))
                    for j, moved in enumerate((pt_dve, pt_act)):
                        pe.wait_ge(moved, upto(w))
                        o = p_ps[j][:, SW:SW + TPB * VW]
                        x = probt[:, ub, j]
                        head = 2 * u + j
                        mm(o[:, 0:VW], x[:, 0:P], v[:, par, 0, head], start=True, stop=True)
                        mm(o[:, VW:], x[:, P:2 * P], v[:, par, 0, head], start=True, stop=False)
                        last = mm(o[:, VW:], x[:, 2 * P:SW], v[:, par, 1, head], start=False, stop=True)
                    last.then_inc(weighed, 1)

                def turn_output(b):
                    pe.wait_ge(at_ready, upto(8 * b + 7, 4))
                    pe.wait_ge(h_done, upto(b - 1))
                    for k in range(TPB):
                        for c in range(DC):
                            last = nc.tensor.transpose(o_ps[:, c * SEQ + k * P:c * SEQ + (k + 1) * P],
                                                       at[:, k, c * P:(c + 1) * P], ident[:])
                    last.then_inc(o_turned, 1)

                def project(b):
                    pe.wait_ge(ot_ready, upto(b))
                    for k in range(TPB):
                        for c in range(DC):
                            last = mm(o_ps[:, k * DM:(k + 1) * DM], ot[:, c, k * P:(k + 1) * P], wo[:, c], start=c == 0,
                                      stop=c == DC - 1)
                    last.then_inc(o_done, 1)

                def pieces(b, par):
                    for u in range(8):
                        piece(b, par, u)
                    scores(0, 0, 0)
                    scores(0, 0, 1)

                def step(b, par, first, last):
                    for u in range(UNITS):
                        turn(b, u)
                        if u < UNITS - 2:
                            scores(b, par, u + 2)
                        elif not last:
                            scores(b + 1, 1 - par, u + 2 - UNITS)
                        if not first and u == 0:
                            turn_output(b - 1)
                        weigh(b, par, u)
                        if not first and u == 1:
                            project(b - 1)
                        if not last:
                            piece(b + 1, 1 - par, u)

                def finish(b):
                    turn_output(b)
                    project(b)

                batches(pe, pieces, step, finish)


def vit_tower(nc, x, log_dt, inv_a, a_imag, b_ri, w_in, conv_w, gamma, beta, gamma_col, beta_col, w_x, a_param, d_param,
              w_out, switch_w, switch_b, f0_w1, f0_b1, f0_w2, f0_b2, w_qkv, w_o, rope, rw, rb, f1_w1, f1_b1, f1_w2,
              f1_b2, out):
    blocks = [NTOK // P + g - 1 for g in (NE, NE + 1)]
    a_neg = nc.dram_tensor("a_neg", (NA * DI,), FP32).ap()
    sorted_x = [nc.dram_tensor(f"sorted_x{i}", (b * P, DM), FP32).ap() for i, b in enumerate(blocks)]
    sorted_y = [nc.dram_tensor(f"sorted_y{i}", (b * P, DM), FP32).ap() for i, b in enumerate(blocks)]
    with ExitStack() as ctx:
        sb, ps, sem = memory(nc, ctx, "tower")
        h = sb("h", [P, NT, DM])
        ident = sb("ident", [P, P])
        ident_h = sb("ident_h", [P, P], BF16)
        strict = sb("strict", [P, P])
        ones = sb("ones", [P, P])
        constants(nc, ctx, ident, ident_h, strict, ones)
        s4_kernel(nc, h, ident, log_dt, inv_a, a_imag, b_ri, x)
        gated_layer(nc, h, ident, w_in, conv_w, gamma, beta, gamma_col, beta_col, w_x, a_param, d_param, w_out, a_neg)
        experts(nc, h, ident, strict, ones, "moe0", switch_w, switch_b, None, NE, f0_w1, f0_b1, f0_w2, f0_b2,
                ACT.Gelu_apprx_tanh, sorted_x[0], sorted_y[0])
        attention(nc, h, ident, ident_h, w_qkv, w_o, rope)
        experts(nc, h, ident, strict, ones, "moe1", rw, rb, CAP, NE + 1, f1_w1, f1_b1, f1_w2, f1_b2,
                ACT.Gelu, sorted_x[1], sorted_y[1], out)


def rope_table():
    inv = (1.0 / 10000.0 ** (np.arange(0, DK, 2, dtype=np.float32) / DK)).astype(np.float32)
    ang = np.arange(SEQ, dtype=np.float32)[:, None] * inv
    cos, sin = np.repeat(np.cos(ang), 2, -1), np.repeat(np.sin(ang), 2, -1)
    sin[:, 0::2] = -sin[:, 0::2]
    return np.stack([cos, sin]).astype(np.float32)


def kernel(**inputs):
    import concourse.bacc as bacc
    from concourse.bass_utils import run_bass_kernel_spmd

    a = {k: np.asarray(v) for k, v in inputs.items()}
    flat = np.ascontiguousarray
    column = lambda v: flat(v.reshape(IC, P).T)
    expert_column = lambda v: flat(v.reshape(-1, FC, P).transpose(0, 2, 1))
    both = lambda w, s: np.concatenate([w, s[None]])
    t, g, f, m, r = "L0_tok_", "L0_attn_", "L0_ffn_", "L1_attn_", "L1_ffn_"
    arrays = {
        "x": a["x"], "log_dt": a[t + "log_dt"], "inv_a": a[t + "inv_A_real"], "a_imag": a[t + "A_imag"],
        "b_ri": a[t + "B_ri"],
        "w_in": a[g + "W_in"], "conv_w": a[g + "conv_w"], "gamma": a[g + "ln_gamma"], "beta": a[g + "ln_beta"],
        "gamma_col": column(a[g + "ln_gamma"]), "beta_col": column(a[g + "ln_beta"]), "w_x": a[g + "W_xproj"],
        "a_param": flat(a[g + "A_param"].T).reshape(P, -1), "d_param": a[g + "D"], "w_out": a[g + "W_out"],
        "switch_w": a[f + "switch_w"], "switch_b": a[f + "switch_b"], "f0_w1": a[f + "w1"],
        "f0_b1": expert_column(a[f + "b1"]), "f0_w2": a[f + "w2"], "f0_b2": a[f + "b2"],
        "w_qkv": np.concatenate([a[m + "Wq"].T, a[m + "Wk"].T, a[m + "Wv"].T], axis=1), "w_o": flat(a[m + "Wo"].T),
        "rope": rope_table(),
        "rw": flat(a[r + "rw"].T), "rb": a[r + "rb"], "f1_w1": both(a[r + "w1"], a[r + "sw1"]),
        "f1_b1": expert_column(both(a[r + "b1"], a[r + "sb1"])), "f1_w2": both(a[r + "w2"], a[r + "sw2"]),
        "f1_b2": both(a[r + "b2"], a[r + "sb2"]),
    }
    nc = bacc.Bacc("TRN2", target_bir_lowering=False, num_devices=1)
    aps = {k: nc.dram_tensor(k, v.shape, FP32, kind="ExternalInput").ap() for k, v in arrays.items()}
    out = nc.dram_tensor("out", (NTOK, DM), FP32, kind="ExternalOutput").ap()
    vit_tower(nc, **aps, out=out)
    got = run_bass_kernel_spmd(nc, [arrays], core_ids=[0])
    return got.results[0]["out"].reshape(NB, SEQ, DM)
```
